# Optimizing a Trainium2 kernel written in Bass

```python
import numpy as np
import jax
import jax.numpy as jnp

def _softmax(x, axis=-1):
    return jax.nn.softmax(x, axis=axis)

def _gelu(x):
    return jax.nn.gelu(x, approximate=True)

def _silu(x):
    return jax.nn.silu(x)

def _sigmoid(x):
    return jax.nn.sigmoid(x)

def _layernorm(x, axis=-1, eps=1e-05):
    m = jnp.mean(x, axis=axis, keepdims=True)
    v = jnp.var(x, axis=axis, keepdims=True)
    return (x - m) / jnp.sqrt(v + eps)

def _scatter_add(tgt, idx, src, axis=0):
    return tgt.at[idx].add(src)

def _segment_sum(src, seg, n):
    return jax.ops.segment_sum(src, seg, n)
kernel_name = 'mk_adj_resnorm_d2_adj_r2_8384bf'

def setup_inputs(seed: int=0):
    np.random.seed(seed)
    _w = jnp.asarray

    def _rec_inputs():
        import jax
        import jax.numpy as jnp
        _gk = jax.random.key(seed)
        x = -0.0005207 + 1.001 * jax.random.normal(jax.random.fold_in(_gk, 1), (8, 2048, 64), jnp.float32)
        _w = (1.0 + jnp.arange(2048, dtype=jnp.float32)) ** (-0.5)
        _w = _w / _w.mean()
        _pij = jnp.clip(0.00390625 * _w[:, None] * _w[None, :], 0.0, 1.0)
        _a = jax.random.uniform(jax.random.fold_in(_gk, 2), (2048, 2048)) < _pij
        adj = _a.astype(jnp.int32)
        return (x, adj)
    x, adj = _rec_inputs()

    def _L0_gnn_setup():
        import jax, jax.numpy as jnp
        import numpy as np
        B, N, FIN, FOUT = (8, 2048, 64, 64)
        NEG_SLOPE = 0.01
        key = jax.random.key(seed)
        k1, k2, k3, k4, k5 = jax.random.split(key, 5)
        inp = jax.random.normal(k1, (B, N, FIN), dtype=jnp.float32)
        adj = jax.random.randint(k2, (N, N), 0, 2, dtype=jnp.int32)
        W_w = jax.random.normal(k3, (FOUT, FIN), dtype=jnp.float32) * (1.0 / np.sqrt(FIN))
        W_b = jax.random.normal(k4, (FOUT,), dtype=jnp.float32) * 0.01
        a = jax.random.normal(k5, (2 * FOUT, N), dtype=jnp.float32) * (1.414 / np.sqrt(2 * FOUT + N))
        return {'inp': inp, 'adj': adj, 'W_w': W_w, 'W_b': W_b, 'a': a}
    _L0_gnn_all = _L0_gnn_setup()
    _L0_gnn_in = {k: v for k, v in _L0_gnn_all.items() if k in ('W_w', 'W_b', 'a')}
    del _L0_gnn_all

    def _L1_gnn_setup():
        import jax, jax.numpy as jnp
        import numpy as np
        NEG = -1e+16
        LN_EPS = 1e-05

        def _gat_layer(h, mask, b):
            scores = jnp.einsum('...nd,...md->...nm', h, h)
            scores = jnp.where(mask, scores, NEG)
            attn = jax.nn.softmax(scores, axis=-1)
            return jnp.einsum('...nm,...md->...nd', attn, h) + b
        key = jax.random.key(seed)
        ks = jax.random.split(key, 6)
        B, N, C, H, D = (8, 1024, 64, 4, 64)
        x = jax.random.normal(ks[0], (B, N, C), dtype=jnp.float32)
        graph = jax.random.randint(ks[1], (N, N), 0, 2, dtype=jnp.int32)
        bnd_h = float(np.sqrt(6.0 / (C + D)))
        Wh = jax.random.uniform(ks[2], (H, D, C), jnp.float32, -bnd_h, bnd_h)
        bh = jnp.zeros((H, D), jnp.float32)
        bnd_o = float(np.sqrt(6.0 / (H * D + D)))
        Wo = jax.random.uniform(ks[3], (D, H * D), jnp.float32, -bnd_o, bnd_o)
        bo = jnp.zeros((D,), jnp.float32)
        gamma = jnp.ones((D,), jnp.float32)
        beta = jnp.zeros((D,), jnp.float32)
        return {'x': x, 'graph': graph, 'Wh': Wh, 'bh': bh, 'Wo': Wo, 'bo': bo, 'gamma': gamma, 'beta': beta}
    _L1_gnn_all = _L1_gnn_setup()
    _L1_gnn_in = {k: v for k, v in _L1_gnn_all.items() if k in ('Wh', 'bh', 'Wo', 'bo', 'gamma', 'beta')}
    del _L1_gnn_all
    return {'x': x, 'adj': adj, 'L0_gnn_W_w': _L0_gnn_in['W_w'], 'L0_gnn_W_b': _L0_gnn_in['W_b'], 'L0_gnn_a': _L0_gnn_in['a'], 'L1_gnn_Wh': _L1_gnn_in['Wh'], 'L1_gnn_bh': _L1_gnn_in['bh'], 'L1_gnn_Wo': _L1_gnn_in['Wo'], 'L1_gnn_bo': _L1_gnn_in['bo'], 'L1_gnn_gamma': _L1_gnn_in['gamma'], 'L1_gnn_beta': _L1_gnn_in['beta']}

def reference(x, adj, L0_gnn_W_w, L0_gnn_W_b, L0_gnn_a, L1_gnn_Wh, L1_gnn_bh, L1_gnn_Wo, L1_gnn_bo, L1_gnn_gamma, L1_gnn_beta):
    import jax
    import jax.numpy as jnp

    def _L0_gnn_ref(inp, adj, W_w, W_b, a):
        import jax, jax.numpy as jnp
        import numpy as np
        B, N, FIN, FOUT = (8, 2048, 64, 64)
        NEG_SLOPE = 0.01
        h = jnp.einsum('bnf,of->bno', inp, W_w) + W_b
        h = h.at[:, 0, :].set(0.0)
        mask = (adj[1:, :] > 0).astype(h.dtype)
        neigh = jnp.einsum('ji,bjf->bif', mask, h[:, :N - 1, :])
        s = jnp.einsum('bif,fi->bi', h, a[:FOUT]) + jnp.einsum('bif,fi->bi', neigh, a[FOUT:])
        s = s.at[:, 0].set(0.0)
        hsum = h.sum(axis=1)
        h_prime = s[:, :, None] * hsum[:, None, :]
        return jnp.where(h_prime >= 0, h_prime, NEG_SLOPE * h_prime)

    def _L1_gnn_ref(x, graph, Wh, bh, Wo, bo, gamma, beta):
        import jax, jax.numpy as jnp
        import numpy as np
        NEG = -1e+16
        LN_EPS = 1e-05

        def _gat_layer(h, mask, b):
            scores = jnp.einsum('...nd,...md->...nm', h, h)
            scores = jnp.where(mask, scores, NEG)
            attn = jax.nn.softmax(scores, axis=-1)
            return jnp.einsum('...nm,...md->...nd', attn, h) + b
        B, N, C = x.shape
        H, D, _ = Wh.shape
        mask = graph + jnp.eye(N, dtype=graph.dtype) > 0
        h = jnp.einsum('bnc,hdc->bhnd', x, Wh)
        out_h = _gat_layer(h, mask[None, None], bh[None, :, None, :])
        cat = jnp.transpose(out_h, (0, 2, 1, 3)).reshape(B, N, H * D)
        z = jax.nn.leaky_relu(cat, negative_slope=0.2)
        h2 = jnp.einsum('bnk,dk->bnd', z, Wo)
        out2 = _gat_layer(h2, mask[None], bo)
        z2 = jax.nn.leaky_relu(out2, negative_slope=0.2)
        mu = jnp.mean(z2, axis=-1, keepdims=True)
        var = jnp.mean(jnp.square(z2 - mu), axis=-1, keepdims=True)
        out = (z2 - mu) * jax.lax.rsqrt(var + LN_EPS) * gamma + beta
        return out
    x = _layernorm(x + _L0_gnn_ref(x, adj, L0_gnn_W_w, L0_gnn_W_b, L0_gnn_a), axis=-1)
    x = _layernorm(x + _L1_gnn_ref(x, adj, L1_gnn_Wh, L1_gnn_bh, L1_gnn_Wo, L1_gnn_bo, L1_gnn_gamma, L1_gnn_beta), axis=-1)
    return x

_drawn_inputs = setup_inputs


def setup_inputs(seed=0):
    import zlib

    import numpy as np

    out = dict(_drawn_inputs(seed))
    spreads = {'L1_gnn_bh': (0.0, 0.1),
     'L1_gnn_bo': (0.0, 0.1),
     'L1_gnn_gamma': (1.0, 0.2),
     'L1_gnn_beta': (0.0, 0.1)}
    factors = {}
    for name, (base, spread) in spreads.items():
        noise = np.random.default_rng([zlib.crc32(name.encode()), seed]).standard_normal(out[name].shape)
        drawn = base * np.exp(spread * noise) if base else spread * noise
        out[name] = jnp.asarray(drawn.astype(out[name].dtype))
    for name, factor in factors.items():
        out[name] = (out[name] * factor).astype(out[name].dtype)
    return out
```

```python
from contextlib import ExitStack, contextmanager

import concourse.bass as bass
from concourse import mybir

ALU = mybir.AluOpType
ACT = mybir.ActivationFunctionType
AX = mybir.AxisListType
F32 = mybir.dt.float32
F16 = mybir.dt.float16
BF16 = mybir.dt.bfloat16
I32 = mybir.dt.int32
U32 = mybir.dt.uint32

P = 128
B, N, D = 8, 2048, 64
H = 4
NT = N // P
BD = B * D
BANK = 512
MASKED_SCORE = 1e16
EPS = 1e-5
LAYER1 = B * H
INSTANCES = LAYER1 + B
OPERAND_DMAS = 7


def build(nc, x, adj, w0, b0, a, wh, bh, wo, bo, gamma, beta, out):
    ctx = ExitStack()
    with ctx:
        def sb(name, shape, dt):
            return ctx.enter_context(nc.sbuf_tensor(name, shape, dt))

        def dram(name, shape, dt):
            return nc.dram_tensor(name, shape, dt, kind="Internal").ap()

        made = {}

        def sem(name):
            if name not in made:
                made[name] = ctx.enter_context(nc.semaphore(name))
            return made[name]

        h_hi_d = dram("h_hi_d", [INSTANCES * D, N], F16)
        h_lo_d = dram("h_lo_d", [INSTANCES * D, N], F16)
        h_d = dram("h_d", [INSTANCES, P, NT * D], F32)
        cat_d = dram("cat_d", [P, B * NT, H * D], F32)
        out2_d = dram("out2_d", [B, P, NT * D], F32)

        mask = sb("mask", [P, NT * N], BF16)
        xs = sb("xs", [P, B * NT * D], F32)
        x_btc = xs[:, :].rearrange("p (b t c) -> p b t c", b=B, t=NT)
        ident = sb("ident", [P, P], F32)
        ident16 = sb("ident16", [P, P], BF16)
        node_on = sb("node_on", [P, NT], F32)
        w_nat = sb("w_nat", [P, 7 * D], F32)
        w0T2 = sb("w0T2", [P, P], F32)
        whT2 = sb("whT2", [P, H * D], F32)
        woT = sb("woT", [P, 2, D], F32)
        bh_col = sb("bh_col", [P, 2], F32)
        rows = sb("rows", [P, 4, D], F32)
        aT = sb("aT", [P, NT, P], F32)
        hsum = sb("hsum", [P, BD], F32)
        s1 = sb("s1", [P, NT, B], F32)
        half_neg = sb("half_neg", [P, NT], F32)
        operands = sb("operands", [P, 3, 2, N], F16)
        q_head = operands[:, 0]
        q_tail = operands[:, 1]
        k_both = operands[:, 2]
        v_rows = sb("v_rows", [P, 2, NT * D], F32)
        scores = sb("scores", [P, 2, N], F32)
        probs = sb("probs", [P, 2, N], F32)
        probsT = sb("probsT", [P, 4, BANK], F32)
        mask_slot = sb("mask_slot", [P, 2, N], BF16)
        outs = sb("outs", [P, 2, NT * D], F32)
        neg_max0 = sb("neg_max0", [P, 2], F32)
        neg_max = sb("neg_max", [P, 2], F32)
        row_sum = sb("row_sum", [P, 2, NT], F32)
        row_inv = sb("row_inv", [P, 2], F32)
        adj_slot = scores[:, :, :].bitcast(I32)
        h_hi = probs[:, :, :].rearrange("p u n -> p (u n)").bitcast(F16)
        h_lo = operands[:, 0:2].rearrange("p a u n -> p (a u n)")
        shifted = k_both[:, 0, 0:2 * BD]
        a_in = v_rows[:, :, :].rearrange("p u n -> p (u n)")
        work = probsT[:, :, :]
        work2 = outs[:, :, :].rearrange("p u n -> p (u n)").rearrange("p (k n) -> p k n", k=4)
        h32 = mask_slot[:, :, :].rearrange("p u n -> p (u n)").bitcast(F32)
        small = sb("small", [P, 4, NT], F32)

        ps = ctx.enter_context(nc.psum_tensor("ps", [P, 8, BANK], F32))

        block = ctx.enter_context(nc.Block())

        def pair(ap):
            return ap.rearrange("p (b c) -> p b c", c=D)

        def attention(first, last, eng, step):
            def head(instance, parity, fresh):
                for t in range(4):
                    def tile(lag, t=t):
                        if t >= lag:
                            return parity, t - lag
                        return None if fresh else (1 - parity, NT + t - lag)
                    step(instance * NT + t, t % 2, instance, t, parity, tile)

            def body(instance, parity):
                with strided(eng, 4, NT, 2) as t:
                    for u in range(2):
                        step(instance * NT + t + u, u, instance, t + u, parity, lambda lag: (parity, t + u - lag))

            head(first, 0, True)
            with strided(eng, first, last - 2, 2) as i:
                for k in range(2):
                    body(i + k, k)
                    head(i + k + 1, 1 - k, False)
            body(last - 2, 0)
            head(last - 1, 1, False)
            body(last - 1, 1)
            for t in range(NT, NT + 3):
                step((last - 1) * NT + t, t % 2, last - 1, None, 1, lambda lag: (1, t - lag) if t - lag < NT else None)

        @contextmanager
        def strided(eng, first, end, by):
            with eng.Fori(first // by, end // by) as i:
                yield i * by

        def col(ap, i, w=1):
            return ap[:, i * w:(i + 1) * w] if isinstance(i, int) else ap[:, bass.ts(i, w)]

        def gate(eng, name):
            eng.sem_inc(sem(f"{name}_gate"), 1)

        def since(eng, s, n):
            if not (isinstance(n, int) and n <= 0):
                eng.wait_ge(s, n)

        def p1_h(u):
            return probs[:, u, 0:2 * H * D].rearrange("p (s n) -> p s n", s=2)

        def p1_hi(u):
            return probs[:, u, 1024:1024 + 256].bitcast(F16).rearrange("p (q n) -> p q n", q=2)

        def p1_lo(u):
            return probs[:, u, 1536:1536 + 256].bitcast(F16).rearrange("p (q n) -> p q n", q=2)

        def p1_x(u):
            return scores[:, u, 0:P]

        def p1_xT(u):
            return scores[:, u, P:2 * P]

        def p2_in(u):
            return scores[:, u, 0:2 * H * D]

        def p2_zT(u):
            return scores[:, u, 512:1024].rearrange("p (k s n) -> p k s n", k=2, s=2)

        def p2_h(u):
            return probs[:, u, 0:2 * D]

        def p2_hi(u):
            return probs[:, u, 128:192].bitcast(F16)

        def p2_lo(u):
            return probs[:, u, 256:320].bitcast(F16)

        f_y, f_c, f_q, f_o = probs[:, 0, 0:1024], probs[:, 0, 1024:2048], probs[:, 1, 0:1024], probs[:, 1, 1024:2048]
        ones16 = k_both[:, 1, 0:P]

        @block.sync
        def _(sp):
            for b in range(B):
                sp.dma_start(xs[:, b * NT * D:(b + 1) * NT * D],
                             x[b].rearrange("(p t) c -> p (t c)", t=NT)).then_inc(sem("x_loaded"), 16)
            sp.dma_start(w_nat[0:D, 0:D], w0).then_inc(sem("weights_loaded"), 16)
            sp.dma_start(w_nat[:, D:3 * D].rearrange("p (k c) -> p k c", k=2),
                         wh.rearrange("(k h) d c -> (h d) k c", k=2)).then_inc(sem("weights_loaded"), 16)
            sp.dma_start(w_nat[0:D, 3 * D:7 * D], wo).then_inc(sem("weights_loaded"), 16)
            sp.dma_start(a_in, a).then_inc(sem("weights_loaded"), 16)
            for k, row in enumerate((b0, bo, gamma, beta)):
                sp.dma_start(rows[:, k, :], row.rearrange("(o c) -> o c", o=1).to_broadcast([P, D])).then_inc(sem("weights_loaded"), 16)
            with nc.allow_non_contiguous_dma(reason="256 bias values, one to a partition"):
                for k in range(2):
                    sp.dma_start(bh_col[:, k:k + 1],
                                 bh.rearrange("(k h) d -> k (h d)", k=2)[k].rearrange("(p o) -> p o", o=1)).then_inc(sem("weights_loaded"), 16)
            def load_adj(t, u):
                sp.dma_start(adj_slot[:, u, :],
                             adj.rearrange("(p t) m -> p (t m)", t=NT)[:, bass.ts(t, N)]).then_inc(sem(f"adj_loaded{u}"), 16)

            load_adj(0, 0)
            load_adj(1, 1)
            with strided(sp, 2, NT, 2) as t:
                for u in range(2):
                    sp.wait_ge(sem("mask_made"), t + u - 1)
                    load_adj(t + u, u)
            sp.wait_ge(sem("lo_made"), NT)
            sp.wait_ge(sem("shift_cleared"), 1)
            sp.wait_ge(sem("hi_made"), NT)
            for lo, hi in ((0, 112), (112, 127)):
                sp.dma_start(shifted[lo + 1:hi + 1, 0:BD], h_hi[lo:hi, (NT - 1) * BD:NT * BD]).then_inc(sem("shifted_in"), 16)
                sp.dma_start(shifted[lo + 1:hi + 1, BD:2 * BD], h_lo[lo:hi, (NT - 1) * BD:NT * BD]).then_inc(sem("shifted_in"), 16)

            with sp.Fori(0, B) as b:
                with strided(sp, 0, NT // 2, 2) as tp:
                    for u in range(2):
                        k = b * (NT // 2) + tp + u
                        sp.wait_ge(sem("p1_h_copied"), k + 1)
                        for h in range(H):
                            sp.dma_start(h_d[b * H + h][:, bass.ts(tp + u, 2 * D)].rearrange("p (s d) -> p s d", s=2),
                                         p1_h(u)[:, :, h * D:(h + 1) * D]).then_inc(sem(f"p1_stored{u}"), 16)
                        sp.wait_ge(sem("p1_lo"), k + 1)
                        for part, d in ((p1_hi, h_hi_d), (p1_lo, h_lo_d)):
                            for q in range(2):
                                sp.dma_start(d[bass.ds(b * (H * D) + q * P, P), bass.ts(tp + u, 2 * P)],
                                             part(u)[:, q, :]).then_inc(sem(f"p1_stored{u}"), 16)
            for u in range(2):
                sp.wait_ge(sem(f"p1_stored{u}"), 16 * 8 * (B * NT // 4))

            def load(instance, parity):
                s = sem(f"operands{parity}")
                rows_ = bass.ds(instance * D, D) if not isinstance(instance, int) else slice(instance * D, instance * D + D)
                for half in range(2):
                    w = slice(half * D, half * D + D)
                    sp.dma_start(q_head[w, parity, :], h_hi_d[rows_, :]).then_inc(s, 16)
                    sp.dma_start(q_tail[w, parity, :], h_lo_d[rows_, :]).then_inc(s, 16)
                    sp.dma_start(k_both[w, parity, :], (h_lo_d if half else h_hi_d)[rows_, :]).then_inc(s, 16)
                sp.dma_start(v_rows[:, parity, :], h_d[instance]).then_inc(s, 16)

            load(0, 0)
            load(1, 1)

            def finished(i, parity):
                sp.wait_ge(sem("normed"), (i + 1) * NT)

            def serve1(b, h, more):
                i = b * H + h
                finished(i, h % 2)
                sp.dma_start(cat_d[:, bass.ts(b, NT), h * D:(h + 1) * D],
                             outs[:, h % 2, :].rearrange("p (t d) -> p t d", t=NT)).then_inc(sem(f"out_stored{h % 2}"), 16)
                if more:
                    load(i + 2, h % 2)

            with sp.Fori(0, B - 1) as b:
                for h in range(H):
                    serve1(b, h, True)
            for h in range(H):
                serve1(B - 1, h, h < 2)
            for u in range(2):
                sp.wait_ge(sem(f"out_stored{u}"), 16 * (LAYER1 // 2))

            def load_cat(k, u):
                sp.dma_start(p2_in(u), cat_d[:, bass.ts(k, 2), :].rearrange("p t d -> p (t d)")).then_inc(sem(f"p2_in{u}"), 16)

            load_cat(0, 0)
            load_cat(1, 1)
            with strided(sp, 2, B * NT // 2, 2) as k:
                for u in range(2):
                    sp.wait_ge(sem("p2_zT"), k + u - 1)
                    load_cat(k + u, u)
            for u in range(2):
                sp.wait_ge(sem(f"p2_stored{u}"), 16 * 5 * (B * NT // 4))
            load(LAYER1, 0)
            load(LAYER1 + 1, 1)

            def serve2(b, u, more):
                finished(b + LAYER1, u)
                sp.dma_start(out2_d[b], outs[:, u, :]).then_inc(sem(f"out_stored{u}"), 16)
                if more:
                    load(b + LAYER1 + 2, u)

            with strided(sp, 0, B - 2, 2) as b:
                for u in range(2):
                    serve2(b + u, u, True)
            for u in range(2):
                serve2(B - 2 + u, u, False)
            for u in range(2):
                sp.wait_ge(sem(f"out_stored{u}"), 16 * (INSTANCES // 2))
            with sp.Fori(0, B) as b:
                sp.dma_start(f_y, out2_d[b]).then_inc(sem("f_in"), 16)
                sp.wait_ge(sem("f_done"), b + 1)
                sp.dma_start(out[b].rearrange("(p t) c -> p (t c)", t=NT), f_o).then_inc(sem("f_stored"), 16)
            sp.wait_ge(sem("f_stored"), 16 * B)

        @block.gpsimd
        def _(pool):
            pool.memset(ident[:, :], 0.0).then_inc(sem("pool_const"), 1)
            pool.memset(node_on[:, :], 1.0).then_inc(sem("pool_const"), 1)
            pool.memset(half_neg[:, :], -0.5).then_inc(sem("pool_const"), 1)
            pool.memset(w0T2[:, :], 0.0).then_inc(sem("w0T2_cleared"), 1)
            pool.memset(shifted[0:1, :], 0.0).then_inc(sem("shift_cleared"), 1)
            pool.wait_ge(sem("pool_const"), 3)
            pool.affine_select(out=ident[:, :], in_=ident[:, :], compare_op=ALU.not_equal, fill=1.0,
                               base=0, pattern=[[-1, P]], channel_multiplier=1).then_inc(sem("pool_const"), 1)
            pool.memset(node_on[0:1, 0:1], 0.0).then_inc(sem("pool_const"), 1)
            pool.wait_ge(sem("pool_const"), 5)
            pool.tensor_copy(ident16[:, :], ident[:, :]).then_inc(sem("pool_const"), 1)
            pool.wait_ge(sem("x_loaded"), 16 * B)
            with strided(pool, 0, NT, 2) as t:
                for u in range(2):
                    pool.wait_ge(sem("xT"), t + u)
                    gate(pool, "pool")
                    pool.tensor_copy(pair(work[:, u, :]), x_btc[:, :, t + u, :]).then_inc(sem("x_staged"), 1)
            with pool.Fori(0, NT) as i:
                pool.wait_ge(sem("a_var"), i + 1)
                pool.tensor_tensor(small[:, 3, 0:B], small[:, 2, 0:B], half_neg[:, 0:B], ALU.pow).then_inc(sem("a_rstd"), 1)
            pool.wait_ge(sem("x1_done"), NT)
            with strided(pool, 0, B * NT // 2, 2) as k:
                for u in range(2):
                    pool.wait_ge(sem("p1_xT"), k + u)
                    gate(pool, "pool")
                    pool.tensor_copy(p1_x(u), col(xs, k + u, P)).then_inc(sem("p1_x"), 1)

            def step(g, u, instance, t, parity, tile):
                if t is None:
                    return
                since(pool, sem("masked1"), g - 1)
                gate(pool, "pool")
                pool.tensor_copy(mask_slot[:, u, :].bitcast(U32), col(mask, t, N).bitcast(U32)).then_inc(sem("mask_staged"), 1)

            pool.wait_ge(sem("mask_ready"), NT)
            attention(0, LAYER1, pool, step)
            with pool.Fori(0, B) as b:
                with strided(pool, 0, NT // 2, 2) as tp:
                    for u in range(2):
                        k = b * (NT // 2) + tp + u
                        pool.wait_ge(sem("p2_h_copied"), k + 1)
                        pool.dma_start(h_d[b + LAYER1][:, bass.ts(tp + u, 2 * D)], p2_h(u)).then_inc(sem(f"p2_stored{u}"), 16)
                        pool.wait_ge(sem("p2_lo"), k + 1)
                        for part, d in ((p2_hi, h_hi_d), (p2_lo, h_lo_d)):
                            for s in range(2):
                                pool.dma_start(d[bass.ds((b + LAYER1) * D, D), bass.ds((tp + u) * (2 * P) + s * P, P)],
                                               part(u)[s * D:(s + 1) * D, :]).then_inc(sem(f"p2_stored{u}"), 16)
            attention(LAYER1, INSTANCES, pool, step)
            with pool.Fori(0, 2 * B) as i:
                pool.wait_ge(sem("f_var"), i + 1)
                pool.tensor_tensor(small[:, 3, :], small[:, 2, :], half_neg[:, :], ALU.pow).then_inc(sem("f_rstd"), 1)

        @block.tensor
        def _(pe):
            pe.wait_ge(sem("pool_const"), 6)
            pe.wait_ge(sem("weights_loaded"), 16 * 10)
            pe.transpose(ps[0:D, 0, 0:D], w_nat[0:D, 0:D], ident[0:D, 0:D])
            for k in range(2):
                pe.transpose(ps[0:D, 0, D + k * P:D + (k + 1) * P], w_nat[:, D + k * D:D + (k + 1) * D], ident[:, :])
            for k in range(2):
                last = pe.transpose(ps[:, 1, k * D:(k + 1) * D], w_nat[0:D, 3 * D + k * P:3 * D + (k + 1) * P], ident[0:D, 0:D])
            last.then_inc(sem("weights_turned"), 1)
            for q in range(4):
                for j in range(4):
                    last = pe.transpose(ps[:, 2 + q, j * P:(j + 1) * P],
                                        a_in.rearrange("f (p t) -> f t p", t=NT)[:, 4 * q + j, :], ident[:, :])
                last.then_inc(sem("a_turned"), 1)
            pe.wait_ge(sem("weights_copied"), 6)
            pe.wait_ge(sem("a_copied"), 4)
            with strided(pe, 0, NT, 2) as t:
                for u in range(2):
                    pe.wait_ge(sem("x_staged"), t + u + 1)
                    for k in range(4):
                        last = pe.transpose(ps[:, 4 + u, k * P:(k + 1) * P], work[:, u, k * P:(k + 1) * P], ident[:, :])
                    last.then_inc(sem("xT"), 1)
                    pe.wait_ge(sem("xT_copied"), t + u + 1)
                    pe.wait_ge(sem("h32"), t + u)
                    for k in range(4):
                        last = pe.matmul(ps[:, 6 + u, k * P:(k + 1) * P], work2[:, u, k * P:(k + 1) * P], w0T2[:, :], start=True, stop=True)
                    last.then_inc(sem("h_ready"), 1)
            pe.wait_ge(sem("hi_made"), NT)
            pe.wait_ge(sem("lo_made"), NT)
            pe.wait_ge(sem("ones_made"), 1)
            for t in range(NT):
                pe.matmul(ps[:, 4, :], ones16, h_hi[:, t * BD:(t + 1) * BD], start=(t == 0), stop=False)
                last = pe.matmul(ps[:, 4, :], ones16, h_lo[:, t * BD:(t + 1) * BD], start=False, stop=(t == NT - 1))
            last.then_inc(sem("hsum_ready"), 1)
            pe.wait_ge(sem("shifted_in"), 16 * 4)
            pe.wait_ge(sem("hsum_copied"), 1)
            with strided(pe, 0, NT // 4, 2) as sweep:
                for u in range(2):
                    pe.wait_ge(sem("neigh_free"), 4 * (sweep + u) + 4)
                    pe.wait_ge(sem("mask_made"), 1)

                    def products(t, hi, lo, start, stop):
                        for j in range(4):
                            m = mask[:, bass.ds(t * N + (sweep + u) * (4 * P) + j * P, P)]
                            pe.matmul(ps[:, 4 * u + j, :], m, hi, start=start, stop=False)
                            last = pe.matmul(ps[:, 4 * u + j, :], m, lo, start=False, stop=stop)
                        return last

                    products(0, shifted[:, 0:BD], shifted[:, BD:2 * BD], True, False)
                    with pe.Fori(1, NT - 1) as t:
                        pe.wait_ge(sem("mask_made"), t + 1)
                        products(t, h_hi[:, bass.ts(t - 1, BD)], h_lo[:, bass.ts(t - 1, BD)], False, False)
                    pe.wait_ge(sem("mask_made"), NT)
                    products(NT - 1, h_hi[:, (NT - 2) * BD:(NT - 1) * BD], h_lo[:, (NT - 2) * BD:(NT - 1) * BD],
                             False, True).then_inc(sem("neigh_ready"), 1)
            pe.wait_ge(sem("x1_done"), NT)
            with strided(pe, 0, B * NT // 2, 2) as k:
                for u in range(2):
                    pe.wait_ge(sem("p1_x"), k + u + 1)
                    pe.wait_ge(sem("p1_xT_copied"), k + u)
                    pe.transpose(ps[:, u, 0:P], p1_x(u), ident[:, :]).then_inc(sem("p1_xT"), 1)
                    pe.wait_ge(sem("p1_xT_copied"), k + u + 1)
                    pe.wait_ge(sem("p1_h_copied"), k + u)
                    for s in range(2):
                        last = pe.matmul(ps[:, 2 + 2 * u + s, 0:H * D], p1_xT(u)[s * D:(s + 1) * D, :],
                                         whT2[s * D:(s + 1) * D, :], start=True, stop=True)
                    last.then_inc(sem("p1_h"), 1)
                    pe.wait_ge(sem("p1_h_copied"), k + u + 1)
                    pe.wait_ge(sem("p1_lo"), k + u)
                    for q in range(2):
                        for s in range(2):
                            last = pe.transpose(ps[:, 6 + u, (2 * q + s) * P:(2 * q + s + 1) * P],
                                                p1_h(u)[:, s, q * P:(q + 1) * P], ident[:, :])
                    last.then_inc(sem("p1_hT"), 1)

            def step(g, u, instance, t, parity, tile):
                def half(c):
                    since(pe, sem(f"masked{c}"), g)
                    for q in range(2):
                        o = ps[:, 2 * c + q, :]
                        w = slice((2 * c + q) * BANK, (2 * c + q + 1) * BANK)
                        k = col(k_both[:, parity], t, P)
                        pe.matmul(o, k, q_head[:, parity, w], start=True, stop=False)
                        last = pe.matmul(o, k, q_tail[:, parity, w], start=False, stop=True)
                    last.then_inc(sem(f"scores{c}"), 1)

                lagged = tile(2)

                def turn(q):
                    bank = 4 + q % 3
                    since(pe, sem(f"turned_copied{(3, 1, 2, 0)[q]}"), g - 1 if q == 3 else g - 2)
                    for j in range(4):
                        c = 4 * q + j
                        last = pe.transpose(ps[:, bank, j * P:(j + 1) * P], probs[:, u, c * P:(c + 1) * P], ident[:, :])
                    last.then_inc(sem(f"turned{q}"), 1)

                def weigh(q, old):
                    pe.wait_ge(sem(f"turned_copied{q}"), g - 1)
                    for j in range(4):
                        c = 4 * q + j
                        last = pe.matmul(ps[:, 7, 0:D], probsT[:, q, j * P:(j + 1) * P],
                                         v_rows[:, old, c * D:(c + 1) * D], start=(c == 0), stop=(c == NT - 1))
                    return last

                if t is not None:
                    if isinstance(t, int) and t == 0:
                        pe.wait_ge(sem(f"operands{parity}"), (instance - parity) * (8 * OPERAND_DMAS) + 16 * OPERAND_DMAS)
                    half(0)
                if lagged:
                    pe.wait_ge(sem("exp_done"), g - 1)
                    turn(0)
                    turn(1)
                    turn(2)
                if t is not None:
                    half(1)
                if lagged:
                    since(pe, sem("normed"), g - 2)
                    weigh(0, lagged[0])
                    turn(3)
                    weigh(1, lagged[0])
                    weigh(2, lagged[0])
                    weigh(3, lagged[0]).then_inc(sem("weighed"), 1)

            attention(0, LAYER1, pe, step)
            with strided(pe, 0, B * NT // 2, 2) as k:
                for u in range(2):
                    pe.wait_ge(sem(f"p2_in{u}"), k * 8 + 16)
                    pe.wait_ge(sem("p2_zT_copied"), k + u)
                    for kk in range(2):
                        for s in range(2):
                            last = pe.transpose(ps[:, u, (2 * kk + s) * P:(2 * kk + s + 1) * P],
                                                p2_in(u)[:, s * H * D + kk * P:s * H * D + (kk + 1) * P], ident[:, :])
                    last.then_inc(sem("p2_zT"), 1)
                    pe.wait_ge(sem("p2_zT_copied"), k + u + 1)
                    pe.wait_ge(sem("p2_h_copied"), k + u)
                    for s in range(2):
                        for kk in range(2):
                            last = pe.matmul(ps[:, 2 + u, s * D:(s + 1) * D], p2_zT(u)[:, kk, s, :], woT[:, kk, :],
                                             start=(kk == 0), stop=(kk == 1))
                    last.then_inc(sem("p2_h"), 1)
                    pe.wait_ge(sem("p2_h_copied"), k + u + 1)
                    pe.wait_ge(sem("p2_lo"), k + u)
                    pe.transpose(ps[:, 4 + u, 0:P], p2_h(u), ident[:, :]).then_inc(sem("p2_hT"), 1)
            attention(LAYER1, INSTANCES, pe, step)

        @block.scalar
        def _(act):
            act.wait_ge(sem("a_turned"), 4)
            for q in range(4):
                act.copy(aT[:, 4 * q:4 * q + 4, :], ps[:, 2 + q, :].rearrange("p (j n) -> p j n", j=4)).then_inc(sem("a_copied"), 1)
            with strided(act, 0, NT, 2) as t:
                for u in range(2):
                    act.wait_ge(sem("xT"), t + u + 1)
                    act.wait_ge(sem("h_ready"), t + u)
                    act.copy(work2[:, u, :], ps[:, 4 + u, :]).then_inc(sem("xT_copied"), 1)
                    act.wait_ge(sem("h32"), t + u + 1)
                    act.activation(h_hi[:, bass.ts(t + u, BD)], h32[:, u * BD:(u + 1) * BD], ACT.Copy,
                                   scale=node_on[:, bass.ds(t + u, 1)]).then_inc(sem("hi_made"), 1)
            act.wait_ge(sem("hsum_ready"), 1)
            act.copy(hsum[:, :], ps[:, 4, :]).then_inc(sem("hsum_copied"), 1)
            with act.Fori(0, NT) as i:
                act.wait_ge(sem("a_centred"), i + 1)
                act.square(work[:, 3, :], work[:, 2, :]).then_inc(sem("a_squared"), 1)
            with strided(act, 0, B * NT // 2, 2) as k:
                for u in range(2):
                    act.wait_ge(sem("p1_xT"), k + u + 1)
                    act.copy(p1_xT(u), ps[:, u, 0:P]).then_inc(sem("p1_xT_copied"), 1)
                    act.wait_ge(sem("p1_h"), k + u + 1)
                    act.wait_ge(sem(f"p1_stored{u}"), k * 64)
                    act.copy(p1_h(u), ps[:, 2 + 2 * u:4 + 2 * u, 0:H * D]).then_inc(sem("p1_h_copied"), 1)
                    act.wait_ge(sem("p1_hT"), k + u + 1)
                    act.copy(p1_hi(u), ps[:, 6 + u, :].rearrange("p (q n) -> p q n", q=2)).then_inc(sem("p1_hi"), 1)

            def step(g, u, instance, t, parity, tile):
                if tile(1):
                    old, tt = tile(1)
                    act.wait_ge(sem("masked1"), g)
                    since(act, sem("turned3"), g - 2)
                    act.activation(probs[:, 1 - u, :], scores[:, 1 - u, :], ACT.Exp, bias=neg_max[:, 1 - u:2 - u], scale=-1.0,
                                   accum_out=col(row_sum[:, old], tt)).then_inc(sem("exp_done"), 1)
                if tile(2):
                    for q in (0, 2):
                        act.wait_ge(sem(f"turned{q}"), g - 1)
                        since(act, sem("weighed"), g - 2)
                        act.copy(probsT[:, q, :], ps[:, 4 + q % 3, :]).then_inc(sem(f"turned_copied{q}"), 1)

            attention(0, LAYER1, act, step)
            with strided(act, 0, B * NT // 2, 2) as k:
                for u in range(2):
                    act.wait_ge(sem("p2_zT"), k + u + 1)
                    for kk in range(2):
                        last = act.activation(p2_zT(u)[:, kk], ps[:, u, kk * 2 * P:(kk + 1) * 2 * P].rearrange("p (s n) -> p s n", s=2),
                                              ACT.Identity, bias=bh_col[:, kk:kk + 1])
                    last.then_inc(sem("p2_biased"), 1)
                    act.wait_ge(sem("p2_h"), k + u + 1)
                    act.wait_ge(sem(f"p2_stored{u}"), k * 40)
                    act.copy(p2_h(u), ps[:, 2 + u, 0:2 * D]).then_inc(sem("p2_h_copied"), 1)
                    act.wait_ge(sem("p2_hT"), k + u + 1)
                    act.copy(p2_hi(u), ps[:, 4 + u, 0:P]).then_inc(sem("p2_hi"), 1)
            attention(LAYER1, INSTANCES, act, step)
            with act.Fori(0, B) as b:
                for k in range(2):
                    act.wait_ge(sem("f_centred"), 2 * b + k + 1)
                    act.square(f_q, f_c).then_inc(sem("f_squared"), 1)

        @block.vector
        def _(dve):
            dve.sem_inc(sem("neigh_free"), 8)
            dve.wait_ge(sem("weights_loaded"), 16 * 10)
            dve.memset(ones16, 1.0).then_inc(sem("ones_made"), 1)
            dve.wait_ge(sem("weights_turned"), 1)
            dve.wait_ge(sem("w0T2_cleared"), 1)
            for k in range(2):
                dve.tensor_copy(w0T2[k * D:(k + 1) * D, k * D:(k + 1) * D], ps[0:D, 0, 0:D]).then_inc(sem("weights_copied"), 1)
                dve.tensor_copy(whT2[k * D:(k + 1) * D, :], ps[0:D, 0, D:D + H * D]).then_inc(sem("weights_copied"), 1)
                dve.tensor_copy(woT[:, k, :], ps[:, 1, k * D:(k + 1) * D]).then_inc(sem("weights_copied"), 1)
            dve.wait_ge(sem("a_copied"), 4)
            b0_all = rows[:, 0:1, :].to_broadcast([P, B, D])
            with strided(dve, 0, NT, 2) as t:
                for u in range(2):
                    dve.wait_ge(sem("h_ready"), t + u + 1)
                    hv = pair(h32[:, u * BD:(u + 1) * BD])
                    dve.tensor_tensor(hv, pair(ps[:, 6 + u, :]), b0_all, ALU.add).then_inc(sem("h32"), 1)
                    dve.wait_ge(sem("h32"), t + u + 1)
                    prod = pair(h32[:, 2 * BD:3 * BD])
                    dve.tensor_tensor(prod, hv, aT[:, bass.ds(t + u, 1), 0:D].to_broadcast([P, B, D]), ALU.mult).then_inc(sem("s1_prod"), 1)
                    dve.wait_ge(sem("s1_prod"), t + u + 1)
                    dve.tensor_reduce(s1[:, t + u, :], prod, AX.X, ALU.add).then_inc(sem("s1_made"), 1)
                    dve.wait_ge(sem("s1_made"), t + u + 1)
                    dve.wait_ge(sem("hi_made"), t + u + 1)
                    dve.scalar_tensor_tensor(h_lo[:, bass.ts(t + u, BD)], h32[:, u * BD:(u + 1) * BD], node_on[:, bass.ds(t + u, 1)],
                                             h_hi[:, bass.ts(t + u, BD)], ALU.mult, ALU.subtract).then_inc(sem("lo_made"), 1)
                    dve.wait_ge(sem(f"adj_loaded{u}"), t * 8 + 16)
                    dve.tensor_scalar(mask[:, bass.ts(t + u, N)].rearrange("p (t q) -> p t q", t=NT),
                                      adj_slot[:, u, :].rearrange("p (q t) -> p t q", t=NT), 0.0, None, ALU.is_gt).then_inc(sem("mask_made"), 1)
            dve.wait_ge(sem("hsum_copied"), 1)
            with strided(dve, 0, NT, 8) as i0:
                for j in range(8):
                    i = i0 + j
                    if j % 4 == 0:
                        dve.wait_ge(sem("neigh_ready"), i0 // 4 + j // 4 + 1)
                    prod = pair(work[:, 0, :])
                    dve.tensor_tensor(prod, pair(ps[:, j, :]), aT[:, bass.ds(i, 1), D:P].to_broadcast([P, B, D]), ALU.mult).then_inc(sem("neigh_free"), 1)
                    dve.wait_ge(sem("neigh_free"), i + 9)
                    dve.tensor_reduce(small[:, 0, 0:B], prod, AX.X, ALU.add).then_inc(sem("s2_made"), 1)
                    dve.wait_ge(sem("s2_made"), i + 1)
                    dve.tensor_tensor(small[:, 1, 0:B], small[:, 0, 0:B], s1[:, i, :], ALU.add).then_inc(sem("s_sum"), 1)
                    dve.wait_ge(sem("s_sum"), i + 1)
                    dve.tensor_scalar(small[:, 1, 0:B], small[:, 1, 0:B], node_on[:, bass.ds(i, 1)], None, ALU.mult).then_inc(sem("s_made"), 1)
                    dve.wait_ge(sem("s_made"), i + 1)
                    y, c = pair(work[:, 1, :]), pair(work[:, 2, :])
                    dve.tensor_tensor(prod, pair(hsum[:, :]), small[:, 1, 0:B].rearrange("p (b o) -> p b o", o=1).to_broadcast([P, B, D]), ALU.mult).then_inc(sem("hp"), 1)
                    dve.wait_ge(sem("hp"), i + 1)
                    dve.scalar_tensor_tensor(work[:, 1, :], work[:, 0, :], 0.01, work[:, 0, :], ALU.mult, ALU.max).then_inc(sem("hp_leaky"), 1)
                    dve.wait_ge(sem("hp_leaky"), i + 1)
                    dve.tensor_tensor(y, y, x_btc[:, :, i, :], ALU.add).then_inc(sem("a_y"), 1)
                    dve.wait_ge(sem("a_y"), i + 1)
                    dve.tensor_reduce(small[:, 0, 0:B], y, AX.X, ALU.add).then_inc(sem("a_mean"), 1)
                    dve.wait_ge(sem("a_mean"), i + 1)
                    dve.scalar_tensor_tensor(c, small[:, 0, 0:B].rearrange("p (b o) -> p b o", o=1).to_broadcast([P, B, D]), -1.0 / D, y,
                                             ALU.mult, ALU.add).then_inc(sem("a_centred"), 1)
                    dve.wait_ge(sem("a_squared"), i + 1)
                    dve.tensor_reduce(small[:, 2, 0:B], pair(work[:, 3, :]), AX.X, ALU.add).then_inc(sem("a_ssq"), 1)
                    dve.wait_ge(sem("a_ssq"), i + 1)
                    dve.tensor_scalar(small[:, 2, 0:B], small[:, 2, 0:B], 1.0 / D, EPS, ALU.mult, ALU.add).then_inc(sem("a_var"), 1)
                    dve.wait_ge(sem("a_rstd"), i + 1)
                    dve.wait_ge(sem("a_centred"), i + 1)
                    dve.tensor_tensor(x_btc[:, :, i, :], c, small[:, 3, 0:B].rearrange("p (b o) -> p b o", o=1).to_broadcast([P, B, D]),
                                      ALU.mult).then_inc(sem("x1_done"), 1)
            with dve.Fori(0, NT) as t:
                d = mask[:, bass.ds(t * (N + P), P)]
                dve.tensor_tensor(d, d, ident16[:, :], ALU.max).then_inc(sem("mask_diag"), 1)
                dve.wait_ge(sem("mask_diag"), t + 1)
                m = mask[:, bass.ts(t, N)]
                dve.tensor_scalar(m, m, -1.0, MASKED_SCORE, ALU.add, ALU.mult).then_inc(sem("mask_ready"), 1)
            with strided(dve, 0, B * NT // 2, 2) as k:
                for u in range(2):
                    dve.wait_ge(sem("p1_hi"), k + u + 1)
                    dve.tensor_tensor(p1_lo(u), ps[:, 6 + u, :].rearrange("p (q n) -> p q n", q=2), p1_hi(u), ALU.subtract).then_inc(sem("p1_lo"), 1)

            def step(g, u, instance, t, parity, tile):
                def masked(c):
                    dve.wait_ge(sem(f"scores{c}"), g + 1)
                    if c == 1:
                        dve.wait_ge(sem("masked0"), g + 1)
                    w = slice(c * 2 * BANK, (c + 1) * 2 * BANK)
                    if c == 0:
                        dve.wait_ge(sem("mask_staged"), g + 1)
                        since(dve, sem("exp_done"), g - 1)
                    gate(dve, "dve")
                    start = 3.0e38 if c == 0 else neg_max0[:, u:u + 1]
                    dve.tensor_tensor_reduce(scores[:, u, w], ps[:, 2 * c:2 * c + 2, :].rearrange("p a n -> p (a n)"), mask_slot[:, u, w],
                                             -1.0, start, ALU.add, ALU.min,
                                             (neg_max0 if c == 0 else neg_max)[:, u:u + 1]).then_inc(sem(f"masked{c}"), 1)

                def copy(q):
                    dve.wait_ge(sem(f"turned{q}"), g - 1)
                    since(dve, sem("weighed"), g - 2)
                    dve.tensor_copy(probsT[:, q, :], ps[:, 4 + q % 3, :]).then_inc(sem(f"turned_copied{q}"), 1)

                if t is not None:
                    masked(0)
                if tile(3):
                    old, tt = tile(3)
                    dve.wait_ge(sem("inverse"), g - 2)
                    dve.wait_ge(sem("weighed"), g - 2)
                    if isinstance(tt, int) and tt == 0:
                        since(dve, sem(f"out_stored{parity}"), (instance - parity) * 8)
                    dve.tensor_scalar(col(outs[:, old], tt, D), ps[:, 7, 0:D], row_inv[:, 1 - u:2 - u], None, ALU.mult).then_inc(sem("normed"), 1)
                if tile(2):
                    copy(1)
                if t is not None:
                    masked(1)
                if tile(2):
                    old, tt = tile(2)
                    dve.reciprocal(row_inv[:, u:u + 1], col(row_sum[:, old], tt)).then_inc(sem("inverse"), 1)
                    copy(3)

            attention(0, LAYER1, dve, step)
            with strided(dve, 0, B * NT // 2, 2) as k:
                for u in range(2):
                    dve.wait_ge(sem("p2_biased"), k + u + 1)
                    z = scores[:, u, 512:1024]
                    dve.scalar_tensor_tensor(z, z, 0.2, z, ALU.mult, ALU.max).then_inc(sem("p2_zT_copied"), 1)
                    dve.wait_ge(sem("p2_hi"), k + u + 1)
                    dve.tensor_tensor(p2_lo(u), ps[:, 4 + u, 0:P], p2_hi(u), ALU.subtract).then_inc(sem("p2_lo"), 1)
            attention(LAYER1, INSTANCES, dve, step)

            def grid(ap):
                return ap.rearrange("p (t c) -> p t c", c=D)

            def spread(ap):
                return ap.rearrange("p (t o) -> p t o", o=1).to_broadcast([P, NT, D])

            def row(k):
                return rows[:, k:k + 1, :].to_broadcast([P, NT, D])

            with dve.Fori(0, B) as b:
                dve.wait_ge(sem("f_in"), 16 * b + 16)
                dve.tensor_tensor(grid(f_y), grid(f_y), row(1), ALU.add).then_inc(sem("f_biased"), 1)
                dve.wait_ge(sem("f_biased"), b + 1)
                dve.scalar_tensor_tensor(f_y, f_y, 0.2, f_y, ALU.mult, ALU.max).then_inc(sem("f_leaky"), 1)
                dve.wait_ge(sem("f_leaky"), b + 1)
                for k in range(2):
                    dve.tensor_reduce(small[:, 0, :], grid(f_y), AX.X, ALU.add).then_inc(sem("f_mean"), 1)
                    dve.wait_ge(sem("f_mean"), 2 * b + k + 1)
                    dve.scalar_tensor_tensor(grid(f_c), spread(small[:, 0, :]), -1.0 / D, grid(f_y), ALU.mult, ALU.add).then_inc(sem("f_centred"), 1)
                    dve.wait_ge(sem("f_squared"), 2 * b + k + 1)
                    dve.tensor_reduce(small[:, 2, :], grid(f_q), AX.X, ALU.add).then_inc(sem("f_ssq"), 1)
                    dve.wait_ge(sem("f_ssq"), 2 * b + k + 1)
                    dve.tensor_scalar(small[:, 2, :], small[:, 2, :], 1.0 / D, EPS, ALU.mult, ALU.add).then_inc(sem("f_var"), 1)
                    dve.wait_ge(sem("f_rstd"), 2 * b + k + 1)
                    dve.wait_ge(sem("f_centred"), 2 * b + k + 1)
                    if k == 0:
                        dve.tensor_tensor(grid(f_y), grid(f_c), spread(small[:, 3, :]), ALU.mult).then_inc(sem("f_normed"), 1)
                        dve.wait_ge(sem("f_normed"), b + 1)
                        dve.tensor_tensor(grid(f_y), grid(f_y), row(2), ALU.mult).then_inc(sem("f_gamma"), 1)
                        dve.wait_ge(sem("f_gamma"), b + 1)
                        dve.tensor_tensor(grid(f_y), grid(f_y), row(3), ALU.add).then_inc(sem("f_beta"), 1)
                        dve.wait_ge(sem("f_beta"), b + 1)
                        dve.tensor_tensor(f_y, f_y, xs[:, bass.ts(b, NT * D)], ALU.add).then_inc(sem("f_residual"), 1)
                        dve.wait_ge(sem("f_residual"), b + 1)
                    else:
                        dve.wait_ge(sem("f_stored"), 16 * b)
                        dve.tensor_tensor(grid(f_o), grid(f_c), spread(small[:, 3, :]), ALU.mult).then_inc(sem("f_done"), 1)


_INS = ['x', 'adj', 'L0_gnn_W_w', 'L0_gnn_W_b', 'L0_gnn_a', 'L1_gnn_Wh', 'L1_gnn_bh', 'L1_gnn_Wo', 'L1_gnn_bo',
        'L1_gnn_gamma', 'L1_gnn_beta']


def kernel(**inputs):
    import numpy as _np
    import concourse.bacc as _bacc
    from concourse import mybir as _mybir
    from concourse.bass_utils import run_bass_kernel_spmd as _run

    nc = _bacc.Bacc("TRN2", target_bir_lowering=False, num_devices=1)
    arrays, args = {}, []
    for name in _INS:
        v = _np.ascontiguousarray(inputs[name])
        arrays[f"in_{name}"] = v
        args.append(nc.dram_tensor(f"in_{name}", v.shape, _mybir.dt.from_np(v.dtype), kind="ExternalInput").ap())
    args.append(nc.dram_tensor("out_0", (B, N, D), F32, kind="ExternalOutput").ap())
    build(nc, *args)
    r = _run(nc, [arrays], core_ids=[0])
    return r.results[0]["out_0"]
```

```python
from contextlib import ExitStack, contextmanager

import concourse.bass as bass
from concourse import mybir

ALU = mybir.AluOpType
ACT = mybir.ActivationFunctionType
AX = mybir.AxisListType
F32 = mybir.dt.float32
F16 = mybir.dt.float16
BF16 = mybir.dt.bfloat16
I32 = mybir.dt.int32
U32 = mybir.dt.uint32

P = 128
B, N, D = 8, 2048, 64
H = 4
NT = N // P
BD = B * D
BANK = 512
SCALE = 32768.0
MASKED_SCORE = 1e16
EPS = 1e-5
LAYER1 = B * H
INSTANCES = LAYER1 + B
OPERAND_DMAS = 6
G = 4
UNITS = B * NT // G
FINISH_STEPS = 40
HALF = NT // 2 * D


def build(nc, x, adj, w0, b0, a, wh, bh, wo, bo, gamma, beta, out):
    ctx = ExitStack()
    with ctx:
        def sb(name, shape, dt):
            return ctx.enter_context(nc.sbuf_tensor(name, shape, dt))

        def dram(name, shape, dt):
            return nc.dram_tensor(name, shape, dt, kind="Internal").ap()

        made = {}

        def sem(name):
            if name not in made:
                made[name] = ctx.enter_context(nc.semaphore(name))
            return made[name]

        hT_d = dram("hT_d", [INSTANCES * P, N], F16)
        h_d = dram("h_d", [P, INSTANCES, NT * P], F16)
        z_d = dram("z_d", [P, LAYER1, NT * P], F16)

        mask = sb("mask", [P, NT * N], BF16)
        xs = sb("xs", [P, B * NT * D], F32)
        x_btc = xs[:, :].rearrange("p (b t c) -> p b t c", b=B, t=NT)
        ident = sb("ident", [P, P], F32)
        ident16 = sb("ident16", [P, P], BF16)
        ident_h = sb("ident_h", [P, P], F16)
        minus = sb("minus", [P, P], BF16)
        node_on = sb("node_on", [P, NT], F32)
        w0T2 = sb("w0T2", [P, P], F32)
        w16 = sb("w16", [P, 2, 2, H * D], F16)
        bh_rows = sb("bh_rows", [P, H, D], F32)
        rows = sb("rows", [P, 4, D], F32)
        hsum = sb("hsum", [P, BD], F32)
        s1 = sb("s1", [P, NT, B], F32)
        half_neg = sb("half_neg", [P, NT], F32)
        operands = sb("operands", [P, 3, 2, N], F16)
        q_head = operands[:, 0]
        q_tail = operands[:, 1]
        k_both = operands[:, 2]
        v_parts = sb("v_parts", [P, 2, NT * P], F16)
        scores = sb("scores", [P, 2, N], F32)
        probs = sb("probs", [P, 2, N], F32)
        probsT = sb("probsT", [P, 2, 2, 4, BANK], F16)
        probsT_hi, probsT_lo = probsT[:, 0], probsT[:, 1]
        mask_slot = sb("mask_slot", [P, 2, N], BF16)
        outs = sb("outs", [P, 2, NT * D], F32)
        scratch = sb("scratch", [P, NT * D], F32)
        z_parts = scratch[:, :].bitcast(F16)
        neg_max0 = sb("neg_max0", [P, 2], F32)
        neg_max = sb("neg_max", [P, 2], F32)
        row_sum = sb("row_sum", [P, 2, NT], F32)
        row_inv = sb("row_inv", [P, 2], F32)
        adj_slot = scores[:, :, :].bitcast(I32)
        h_hi = probs[:, :, :].rearrange("p u n -> p (u n)").bitcast(F16)
        h_lo = operands[:, 0:2].rearrange("p a u n -> p (a u n)")
        shifted = k_both[:, 0, 0:2 * BD]
        a_in = v_parts[:, :, :].rearrange("p u n -> p (u n)").bitcast(F32)
        work = probsT[:, 0].rearrange("p a k n -> p (a k n)").bitcast(F32).rearrange("p (k n) -> p k n", k=4)
        work2 = outs[:, :, :].rearrange("p u n -> p (u n)").rearrange("p (k n) -> p k n", k=4)
        h32 = mask_slot[:, :, :].rearrange("p u n -> p (u n)").bitcast(F32)
        aT = probsT[:, 1].rearrange("p a k n -> p (a k n)").bitcast(F32).rearrange("p (t f) -> p t f", t=NT)
        w_nat = scratch[:, 0:7 * D]
        small = sb("small", [P, 4, NT], F32)
        stats = sb("stats", [P, 3, NT // 2], F32)

        ps = ctx.enter_context(nc.psum_tensor("ps", [P, 8, BANK], F32))

        block = ctx.enter_context(nc.Block())

        def pair(ap):
            return ap.rearrange("p (b c) -> p b c", c=D)

        def attention(first, last, eng, step):
            def head(instance, parity, fresh):
                for t in range(2):
                    def tile(lag, t=t):
                        if t >= lag:
                            return parity, t - lag
                        return None if fresh else (1 - parity, NT + t - lag)
                    step(instance * NT + t, t % 2, instance, t, parity, tile)

            def body(instance, parity):
                with strided(eng, 2, NT, 2) as t:
                    for u in range(2):
                        step(instance * NT + t + u, u, instance, t + u, parity, lambda lag: (parity, t + u - lag))

            head(first, 0, True)
            with strided(eng, first, last - 2, 2) as i:
                for k in range(2):
                    body(i + k, k)
                    head(i + k + 1, 1 - k, False)
            body(last - 2, 0)
            head(last - 1, 1, False)
            body(last - 1, 1)
            for t in range(NT, NT + 2):
                step((last - 1) * NT + t, t % 2, last - 1, None, 1, lambda lag: (1, t - lag) if t - lag < NT else None)

        @contextmanager
        def strided(eng, first, end, by):
            with eng.Fori(first // by, end // by) as i:
                yield i * by

        def col(ap, i, w=1):
            return ap[:, i * w:(i + 1) * w] if isinstance(i, int) else ap[:, bass.ts(i, w)]

        def gate(eng, name):
            eng.sem_inc(sem(f"{name}_gate"), 1)

        def since(eng, s, n):
            if not (isinstance(n, int) and n <= 0):
                eng.wait_ge(s, n)

        def stage16(buffer, u, at, n):
            return buffer[:, u, at // 2:(at + n) // 2].bitcast(F16)

        def x_parts(u):
            return stage16(scores, u, 0, G * P).rearrange("p (s k c) -> p s k c", s=G, k=2)

        def xT_parts(u):
            return stage16(scores, u, G * P, G * P)

        def z_in(u):
            return stage16(scores, u, 0, H * G * P)

        def zT_parts(u):
            return stage16(scores, u, H * G * P // 2 * 2, H * G * P)

        def h_parts(u):
            return stage16(probs, u, 0, H * G * P)

        def hT_parts(u):
            return stage16(probs, u, H * G * P, H * G * P)

        def banks16(bank, n):
            return ps[:, bank:bank + n, :].rearrange("p a n -> p (a n)").bitcast(F16)

        def units(eng, step):
            step(0, 0)
            step(1, 1)
            with strided(eng, 2, UNITS - 2, 2) as k:
                for u in range(2):
                    step(k + u, u)
            step(UNITS - 2, 0)
            step(UNITS - 1, 1)

        def within(k):
            return not isinstance(k, int) or 0 <= k < UNITS

        ones16 = k_both[:, 1, 0:P]
        TURN_BANK = (4, 5, 6, 5)

        def products(u):
            return ps[:, 2 + 2 * u:4 + 2 * u, :].rearrange("p a n -> p (a n)").rearrange("p (s h d) -> p s h d", s=G, h=H)

        def by_tiles(parts, part):
            return parts.rearrange("p (h s k d) -> p s h k d", h=H, s=G, k=2)[:, :, :, part, :]

        def tile_part(u, part):
            return h_parts(u)[:, 0:G * P].rearrange("p (s k d) -> p s k d", s=G, k=2)[:, :, part, :]

        def stores(k, u):
            return (k - u) * 8

        def half_x1(c):
            return col(xs, c, HALF)

        def half_out(b, half):
            return out[b].rearrange("(p t) c -> p (t c)", t=NT)[:, half * HALF:(half + 1) * HALF]

        def finish(eng, c, y, name):
            last = name == "last"
            n = 1 if last else c + 1
            x1 = half_x1(c)
            squares = scratch[:, 0:HALF]

            def grid(ap):
                return ap.rearrange("p (t c) -> p t c", c=D)

            def spread(k):
                return stats[:, k, :].rearrange("p (t o) -> p t o", o=1).to_broadcast([P, NT // 2, D])

            def row(k):
                return rows[:, k:k + 1, :].to_broadcast([P, NT // 2, D])

            steps = []

            def then(instruction):
                steps.append(1)
                instruction.then_inc(sem(f"{name}_step"), 1)
                eng.wait_ge(sem(f"{name}_step"), len(steps) if last else c * FINISH_STEPS + len(steps))
                gate(eng, name)

            def signal(what, instruction, n):
                instruction.then_inc(sem(f"{name}_{what}"), 1)
                eng.wait_ge(sem(f"{name}_{what}"), n)
                gate(eng, name)

            def total(v, k):
                if last:
                    then(eng.tensor_reduce(stats[:, k, :], grid(v), AX.X, ALU.add))
                    return
                w, v, s = D // 2, grid(v), grid(squares)
                while w:
                    o = s[:, :, 0:w] if w > 1 else stats[:, k, :].rearrange("p (t o) -> p t o", o=1)
                    then(eng.tensor_tensor(o, v[:, :, 0:w], v[:, :, w:2 * w], ALU.add))
                    v, w = s, w // 2

            def centred(v, k):
                total(v, 0)
                then(eng.tensor_scalar(stats[:, 0, :], stats[:, 0, :], -1.0 / D, 0.0, ALU.mult, ALU.add))
                then(eng.tensor_tensor(grid(v), grid(v), spread(0), ALU.add))
                then(eng.tensor_tensor(squares, v, v, ALU.mult))
                total(squares, 1)
                var = eng.tensor_scalar(stats[:, 1, :], stats[:, 1, :], 1.0 / D, EPS, ALU.mult, ALU.add)
                if last:
                    signal("var", var, k + 1)
                    eng.wait_ge(sem("last_rstd"), k + 1)
                else:
                    then(var)
                    then(eng.tensor_tensor(stats[:, 2, :], stats[:, 1, :], half_neg[:, 0:NT // 2], ALU.pow))

            then(eng.tensor_tensor(grid(y), grid(y), row(1), ALU.add))
            then(eng.tensor_scalar(squares, y, 0.0, -0.8, ALU.min, ALU.mult))
            then(eng.tensor_tensor(y, y, squares, ALU.add))
            centred(y, 0)
            then(eng.tensor_tensor(grid(y), grid(y), spread(2), ALU.mult))
            then(eng.tensor_tensor(grid(y), grid(y), row(2), ALU.mult))
            then(eng.tensor_tensor(grid(y), grid(y), row(3), ALU.add))
            signal("residual", eng.tensor_tensor(x1, x1, y, ALU.add), n)
            centred(x1, 1)
            signal("done", eng.tensor_tensor(grid(x1), grid(x1), spread(2), ALU.mult), n)
            assert last or len(steps) == FINISH_STEPS

        @block.sync
        def _(sp):
            for b in range(B):
                sp.dma_start(xs[:, b * NT * D:(b + 1) * NT * D],
                             x[b].rearrange("(p t) c -> p (t c)", t=NT)).then_inc(sem("x_loaded"), 16)
            sp.dma_start(w_nat[0:D, 0:D], w0).then_inc(sem("weights_loaded"), 16)
            sp.dma_start(w_nat[:, D:3 * D].rearrange("p (k c) -> p k c", k=2),
                         wh.rearrange("(k h) d c -> (h d) k c", k=2)).then_inc(sem("weights_loaded"), 16)
            sp.dma_start(w_nat[0:D, 3 * D:7 * D], wo).then_inc(sem("weights_loaded"), 16)
            sp.dma_start(bh_rows[:, :, :].rearrange("p h d -> p (h d)"),
                         bh.rearrange("h d -> (h d)").rearrange("(o n) -> o n", o=1).to_broadcast([P, H * D])).then_inc(sem("weights_loaded"), 16)
            sp.dma_start(a_in, a).then_inc(sem("weights_loaded"), 16)
            for k, row in enumerate((b0, bo, gamma, beta)):
                sp.dma_start(rows[:, k, :], row.rearrange("(o c) -> o c", o=1).to_broadcast([P, D])).then_inc(sem("weights_loaded"), 16)
            def load_adj(t, u):
                sp.dma_start(adj_slot[:, u, :],
                             adj.rearrange("(p t) m -> p (t m)", t=NT)[:, bass.ts(t, N)]).then_inc(sem(f"adj_loaded{u}"), 16)

            load_adj(0, 0)
            load_adj(1, 1)
            with strided(sp, 2, NT, 2) as t:
                for u in range(2):
                    sp.wait_ge(sem("mask_made"), t + u - 1)
                    load_adj(t + u, u)
            sp.wait_ge(sem("lo_made"), NT)
            sp.wait_ge(sem("shift_cleared"), 1)
            sp.wait_ge(sem("hi_made"), NT)
            for lo, hi in ((0, 112), (112, 127)):
                sp.dma_start(shifted[lo + 1:hi + 1, 0:BD], h_hi[lo:hi, (NT - 1) * BD:NT * BD]).then_inc(sem("shifted_in"), 16)
                sp.dma_start(shifted[lo + 1:hi + 1, BD:2 * BD], h_lo[lo:hi, (NT - 1) * BD:NT * BD]).then_inc(sem("shifted_in"), 16)

            with sp.Fori(0, B) as b:
                for j in range(NT // G):
                    u = j % 2
                    k = b * (NT // G) + j
                    sp.wait_ge(sem("p1_lo"), k + 1)
                    sp.dma_start(h_d[:, bass.ts(b, H), j * G * P:(j + 1) * G * P],
                                 h_parts(u).rearrange("p (h n) -> p h n", h=H)).then_inc(sem(f"h_stored{u}"), 16)
                    sp.wait_ge(sem("p1_hT_a"), k + 1)
                    sp.wait_ge(sem("p1_hT_b"), k + 1)
                    sp.dma_start(hT_d[bass.ts(b, H * P), j * G * P:(j + 1) * G * P].rearrange("(h q) n -> q h n", h=H),
                                 hT_parts(u).rearrange("p (h n) -> p h n", h=H)).then_inc(sem(f"hT_stored{u}"), 16)
            for u in range(2):
                sp.wait_ge(sem(f"h_stored{u}"), 8 * UNITS)
                sp.wait_ge(sem(f"hT_stored{u}"), 8 * UNITS)

            def load(i, parity):
                s = sem(f"operands{parity}")

                def part(k):
                    at = i * P + k * D
                    return hT_d[at:at + D, :] if isinstance(i, int) else hT_d[bass.ds(at, D), :]

                for half in range(2):
                    w = slice(half * D, half * D + D)
                    sp.dma_start(q_head[w, parity, :], part(0)).then_inc(s, 16)
                    sp.dma_start(q_tail[w, parity, :], part(1)).then_inc(s, 16)
                sp.dma_start(k_both[:, parity, :], hT_d[i * P:(i + 1) * P, :] if isinstance(i, int) else hT_d[bass.ts(i, P), :]).then_inc(s, 16)
                sp.dma_start(v_parts[:, parity, :], h_d[:, i, :] if isinstance(i, int) else h_d[:, bass.ds(i, 1), :]).then_inc(s, 16)

            load(0, 0)
            load(1, 1)

            def step(g, u, instance, t, parity, tile):
                if t is None:
                    return
                if not (isinstance(g, int) and g == 0):
                    sp.wait_ge(sem("masked1"), g)
                    gate(sp, "sp")
                sp.dma_start(mask_slot[:, 1 - u, :], col(mask, (t + 1) % NT, N)).then_inc(sem(f"mask_staged{1 - u}"), 16)
                if isinstance(t, int) and t == 1 and tile(2) and more(instance):
                    sp.wait_ge(sem("normed"), instance * NT)
                    gate(sp, "sp")
                    load(instance + 1, 1 - parity)

            def more(instance):
                return not isinstance(instance, int) or instance not in (LAYER1 - 1, INSTANCES - 1)

            sp.wait_ge(sem("mask_ready"), NT)
            sp.dma_start(mask_slot[:, 0, :], mask[:, 0:N]).then_inc(sem("mask_staged0"), 16)
            attention(0, LAYER1, sp, step)
            sp.wait_ge(sem("z_stored"), 16 * LAYER1)

            def load_z(b, j):
                sp.dma_start(z_in(j % 2).rearrange("p (h n) -> p h n", h=H),
                             z_d[:, b * H:(b + 1) * H, j * G * P:(j + 1) * G * P] if isinstance(b, int) else
                             z_d[:, bass.ts(b, H), j * G * P:(j + 1) * G * P]).then_inc(sem(f"z_in{j % 2}"), 16)

            load_z(0, 0)
            load_z(0, 1)

            def serve_units(b, last):
                for j in range(NT // G):
                    u = j % 2
                    k = b * (NT // G) + j
                    if not (last and j >= 2):
                        sp.wait_ge(sem("p2_zT"), k + 1)
                        load_z(b + j // 2, (j + 2) % (NT // G))
                    sp.wait_ge(sem("p2_lo"), k + 1)
                    sp.dma_start(h_d[:, LAYER1 + b, j * G * P:(j + 1) * G * P] if isinstance(b, int) else
                                 h_d[:, bass.ds(b + LAYER1, 1), j * G * P:(j + 1) * G * P],
                                 h_parts(u)[:, 0:G * P]).then_inc(sem(f"h2_stored{u}"), 16)
                    sp.wait_ge(sem("p2_hT"), k + 1)
                    sp.dma_start(hT_d[(LAYER1 + b) * P:(LAYER1 + b + 1) * P, j * G * P:(j + 1) * G * P] if isinstance(b, int) else
                                 hT_d[bass.ts(b + LAYER1, P), j * G * P:(j + 1) * G * P],
                                 hT_parts(u)[:, 0:G * P]).then_inc(sem(f"h2T_stored{u}"), 16)

            with sp.Fori(0, B - 1) as b:
                serve_units(b, False)
            serve_units(B - 1, True)
            for u in range(2):
                sp.wait_ge(sem(f"h2_stored{u}"), 8 * UNITS)
                sp.wait_ge(sem(f"h2T_stored{u}"), 8 * UNITS)
            load(LAYER1, 0)
            load(LAYER1 + 1, 1)

            attention(LAYER1, INSTANCES, sp, step)
            sp.wait_ge(sem("mask_staged0"), 16 * (INSTANCES * NT // 2 + 1))
            sp.wait_ge(sem("last_done"), 1)
            sp.dma_start(half_out(B - 1, 1), half_x1(2 * B - 1)).then_inc(sem("last_stored"), 16)
            sp.wait_ge(sem("last_stored"), 16)

        @block.gpsimd
        def _(pool):
            pool.memset(ident[:, :], 0.0).then_inc(sem("pool_const"), 1)
            pool.memset(node_on[:, :], 1.0).then_inc(sem("pool_const"), 1)
            pool.memset(half_neg[:, :], -0.5).then_inc(sem("pool_const"), 1)
            pool.memset(w0T2[:, :], 0.0).then_inc(sem("w0T2_cleared"), 1)
            pool.memset(shifted[0:1, :], 0.0).then_inc(sem("shift_cleared"), 1)
            pool.wait_ge(sem("pool_const"), 3)
            pool.affine_select(out=ident[:, :], in_=ident[:, :], compare_op=ALU.not_equal, fill=1.0,
                               base=0, pattern=[[-1, P]], channel_multiplier=1).then_inc(sem("pool_const"), 1)
            pool.memset(node_on[0:1, 0:1], 0.0).then_inc(sem("pool_const"), 1)
            pool.wait_ge(sem("pool_const"), 5)
            pool.tensor_copy(ident16[:, :], ident[:, :]).then_inc(sem("pool_const"), 1)
            pool.tensor_copy(ident_h[:, :], ident[:, :]).then_inc(sem("pool_const"), 1)
            pool.tensor_scalar(minus[:, :], ident[:, :], -1.0 / SCALE, 0.0, ALU.mult, ALU.add).then_inc(sem("pool_const"), 1)
            pool.wait_ge(sem("x_loaded"), 16 * B)
            with strided(pool, 0, NT, 2) as t:
                for u in range(2):
                    pool.wait_ge(sem("xT"), t + u)
                    gate(pool, "pool")
                    pool.tensor_copy(pair(work[:, u, :]), x_btc[:, :, t + u, :]).then_inc(sem("x_staged"), 1)
            with pool.Fori(0, NT) as i:
                pool.wait_ge(sem("a_var"), i + 1)
                pool.tensor_tensor(small[:, 3, 0:B], small[:, 2, 0:B], half_neg[:, 0:B], ALU.pow).then_inc(sem("a_rstd"), 1)
            pool.wait_ge(sem("x1_done"), NT)

            def part_step(k, u):
                since(pool, sem("p1_xT"), k - 1)
                gate(pool, "pool")
                x1 = col(xs, k, G * D).rearrange("p (s c) -> p s c", s=G)
                pool.tensor_copy(x_parts(u)[:, :, 0, :], x1).then_inc(sem("x1_hi"), 1)
                pool.wait_ge(sem("x1_hi"), k + 1)
                gate(pool, "pool")
                pool.tensor_tensor(x_parts(u)[:, :, 1, :], x1, x_parts(u)[:, :, 0, :], ALU.subtract).then_inc(sem("x1_lo"), 1)

            units(pool, part_step)

            with pool.Fori(0, B) as b:
                for h in range(H):
                    i = b * H + h
                    z = outs[:, h % 2, :]
                    zv = z.rearrange("p (t d) -> p t d", t=NT)
                    parts = z_parts.rearrange("p (t k d) -> p t k d", t=NT, k=2)
                    pool.wait_ge(sem("normed"), (i + 1) * NT)
                    gate(pool, "pool")
                    pool.tensor_tensor(zv, zv, bh_rows[:, h:h + 1, :].to_broadcast([P, NT, D]), ALU.add).then_inc(sem("z_biased"), 1)
                    pool.wait_ge(sem("z_biased"), i + 1)
                    gate(pool, "pool")
                    pool.wait_ge(sem("z_stored"), i * 16)
                    gate(pool, "pool")
                    pool.tensor_scalar(scratch[:, :], z, 0.0, -0.8, ALU.min, ALU.mult).then_inc(sem("z_scaled"), 1)
                    pool.wait_ge(sem("z_scaled"), i + 1)
                    gate(pool, "pool")
                    pool.tensor_tensor(z, z, scratch[:, :], ALU.add).then_inc(sem("z_leaky"), 1)
                    pool.wait_ge(sem("z_leaky"), i + 1)
                    gate(pool, "pool")
                    pool.tensor_copy(parts[:, :, 0, :], zv).then_inc(sem("z_hi"), 1)
                    pool.wait_ge(sem("z_hi"), i + 1)
                    gate(pool, "pool")
                    pool.tensor_tensor(parts[:, :, 1, :], zv, parts[:, :, 0, :], ALU.subtract).then_inc(sem("z_lo"), 1)
                    pool.wait_ge(sem("z_lo"), i + 1)
                    gate(pool, "pool")
                    pool.dma_start(z_d[:, bass.ds(i, 1), :], z_parts).then_inc(sem("z_stored"), 16)

            def half_batch(b, u, half):
                c = 2 * b + half
                pool.wait_ge(sem("normed"), (b + LAYER1) * NT + (half + 1) * (NT // 2))
                gate(pool, "pool")
                finish(pool, c, outs[:, u, half * HALF:(half + 1) * HALF], "f")
                pool.dma_start(half_out(b, half), half_x1(c)).then_inc(sem("out_stored"), 16)

            pool.wait_ge(sem("z_stored"), 16 * LAYER1)
            with strided(pool, 0, B - 2, 2) as b:
                for u in range(2):
                    for half in range(2):
                        half_batch(b + u, u, half)
            half_batch(B - 2, 0, 0)
            half_batch(B - 2, 0, 1)
            half_batch(B - 1, 1, 0)
            for k in range(2):
                pool.wait_ge(sem("last_var"), k + 1)
                pool.tensor_tensor(stats[:, 2, :], stats[:, 1, :], half_neg[:, 0:NT // 2], ALU.pow).then_inc(sem("last_rstd"), 1)
            pool.wait_ge(sem("out_stored"), 16 * (2 * B - 1))

        @block.tensor
        def _(pe):
            pe.wait_ge(sem("pool_const"), 8)
            pe.wait_ge(sem("weights_loaded"), 16 * 9)
            pe.transpose(ps[0:D, 0, 0:D], w_nat[0:D, 0:D], ident[0:D, 0:D])
            for k in range(2):
                pe.transpose(ps[0:D, 0, D + k * P:D + (k + 1) * P], w_nat[:, D + k * D:D + (k + 1) * D], ident[:, :])
            for k in range(H):
                last = pe.transpose(ps[0:D, 1, k * D:(k + 1) * D], w_nat[0:D, 3 * D + k * D:3 * D + (k + 1) * D], ident[0:D, 0:D])
            last.then_inc(sem("weights_turned"), 1)
            for q in range(4):
                for j in range(4):
                    last = pe.transpose(ps[:, 2 + q, j * P:(j + 1) * P],
                                        a_in.rearrange("f (p t) -> f t p", t=NT)[:, 4 * q + j, :], ident[:, :])
                last.then_inc(sem("a_turned"), 1)
            pe.wait_ge(sem("weights_copied"), 2)
            pe.wait_ge(sem("a_copied"), 4)
            with strided(pe, 0, NT, 2) as t:
                for u in range(2):
                    pe.wait_ge(sem("x_staged"), t + u + 1)
                    for k in range(4):
                        last = pe.transpose(ps[:, 4 + u, k * P:(k + 1) * P], work[:, u, k * P:(k + 1) * P], ident[:, :])
                    last.then_inc(sem("xT"), 1)
                    pe.wait_ge(sem("xT_copied"), t + u + 1)
                    pe.wait_ge(sem("h32"), t + u)
                    for k in range(4):
                        last = pe.matmul(ps[:, 6 + u, k * P:(k + 1) * P], work2[:, u, k * P:(k + 1) * P], w0T2[:, :], start=True, stop=True)
                    last.then_inc(sem("h_ready"), 1)
            pe.wait_ge(sem("hi_made"), NT)
            pe.wait_ge(sem("lo_made"), NT)
            pe.wait_ge(sem("ones_made"), 1)
            for t in range(NT):
                pe.matmul(ps[:, 4, :], ones16, h_hi[:, t * BD:(t + 1) * BD], start=(t == 0), stop=False)
                last = pe.matmul(ps[:, 4, :], ones16, h_lo[:, t * BD:(t + 1) * BD], start=False, stop=(t == NT - 1))
            last.then_inc(sem("hsum_ready"), 1)
            pe.wait_ge(sem("shifted_in"), 16 * 4)
            pe.wait_ge(sem("hsum_copied"), 1)
            with strided(pe, 0, NT // 4, 2) as sweep:
                for u in range(2):
                    pe.wait_ge(sem("neigh_free"), 4 * (sweep + u) + 4)
                    pe.wait_ge(sem("mask_made"), 1)

                    def products(t, hi, lo, start, stop):
                        for j in range(4):
                            m = mask[:, bass.ds(t * N + (sweep + u) * (4 * P) + j * P, P)]
                            pe.matmul(ps[:, 4 * u + j, :], m, hi, start=start, stop=False)
                            last = pe.matmul(ps[:, 4 * u + j, :], m, lo, start=False, stop=stop)
                        return last

                    products(0, shifted[:, 0:BD], shifted[:, BD:2 * BD], True, False)
                    with pe.Fori(1, NT - 1) as t:
                        pe.wait_ge(sem("mask_made"), t + 1)
                        products(t, h_hi[:, bass.ts(t - 1, BD)], h_lo[:, bass.ts(t - 1, BD)], False, False)
                    pe.wait_ge(sem("mask_made"), NT)
                    products(NT - 1, h_hi[:, (NT - 2) * BD:(NT - 1) * BD], h_lo[:, (NT - 2) * BD:(NT - 1) * BD],
                             False, True).then_inc(sem("neigh_ready"), 1)
            def turn_x1(k, u):
                since(pe, sem("x1_lo"), k + 1)
                since(pe, sem("p1_xT_copied"), k - 1)
                for s in range(G):
                    last = pe.transpose(banks16(u, 1)[:, s * P:(s + 1) * P],
                                        x_parts(u).rearrange("p s k c -> p s (k c)")[:, s, :], ident_h[:, :])
                last.then_inc(sem("p1_xT"), 1)

            def turn_h(k, u):
                pe.wait_ge(sem("p1_lo"), k + 1)
                since(pe, sem("p1_hT_a"), k)
                since(pe, sem("p1_hT_b"), k)
                for c in range(H * G):
                    last = pe.transpose(banks16(6, 2)[:, c * P:(c + 1) * P], h_parts(u)[:, c * P:(c + 1) * P], ident_h[:, :])
                last.then_inc(sem("p1_hT"), 1)

            def p1_step(k, u):
                pe.wait_ge(sem("p1_xT_copied"), k + 1)
                since(pe, sem("p1_lo"), k - 1)
                for s in range(G):
                    o = ps[:, 2 + 2 * u + s // 2, (s % 2) * H * D:(s % 2 + 1) * H * D]
                    for part in range(2):
                        last = pe.matmul(o, xT_parts(u)[:, s * P:(s + 1) * P], w16[:, 0, part, :], start=(part == 0), stop=(part == 1))
                last.then_inc(sem("p1_h"), 1)
                if within(k + 1):
                    turn_x1(k + 1, 1 - u)
                if within(k - 1):
                    turn_h(k - 1, 1 - u)

            pe.wait_ge(sem("x1_done"), NT)
            turn_x1(0, 0)
            units(pe, p1_step)
            turn_h(UNITS - 1, 1)

            def step(g, u, instance, t, parity, tile):
                def half(c):
                    since(pe, sem(f"masked{c}"), g)
                    for q in range(2):
                        o = ps[:, 2 * c + q, :]
                        w = slice((2 * c + q) * BANK, (2 * c + q + 1) * BANK)
                        k = col(k_both[:, parity], t, P)
                        pe.matmul(o, k, q_head[:, parity, w], start=True, stop=False)
                        last = pe.matmul(o, k, q_tail[:, parity, w], start=False, stop=True)
                    last.then_inc(sem(f"scores{c}"), 1)

                new, old = tile(1), tile(2)

                def turn(q, slot):
                    for j in range(4):
                        c = 4 * q + j
                        last = pe.matmul(ps[:, TURN_BANK[q], j * P:(j + 1) * P], probs[:, slot, c * P:(c + 1) * P], ident[:, :],
                                         start=(j == 0), stop=(j == 3), is_transpose=True, skip_group_check=True)
                    last.then_inc(sem(f"turned{q}"), 1)

                def weigh(q):
                    pe.wait_ge(sem(f"part_lo{q}"), g - 1)
                    for j in range(4):
                        c = 4 * q + j
                        w, v, v_tail = slice(j * P, (j + 1) * P), slice(c * P, c * P + D), slice(c * P + D, (c + 1) * P)
                        hi, lo = probsT_hi[:, u, q, w], probsT_lo[:, u, q, w]
                        pe.matmul(ps[:, 7, 0:D], hi, v_parts[:, old[0], v], start=(c == 0), stop=False)
                        pe.matmul(ps[:, 7, 0:D], hi, v_parts[:, old[0], v_tail], start=False, stop=False)
                        last = pe.matmul(ps[:, 7, 0:D], lo, v_parts[:, old[0], v], start=False, stop=(c == NT - 1))
                    return last

                if t is not None:
                    if isinstance(t, int) and t == 0:
                        pe.wait_ge(sem(f"operands{parity}"), (instance - parity) * (8 * OPERAND_DMAS) + 16 * OPERAND_DMAS)
                    half(0)
                if old:
                    pe.wait_ge(sem("part_lo1"), g - 1)
                    turn(3, u)
                if t is not None:
                    half(1)
                if new:
                    pe.wait_ge(sem("exp_done"), g)
                    since(pe, sem("part_lo0"), g - 1)
                    turn(0, 1 - u)
                    since(pe, sem("part_lo2"), g - 1)
                    turn(2, 1 - u)
                if old:
                    since(pe, sem("normed"), g - 2)
                    weigh(0)
                if new:
                    since(pe, sem("part_lo3"), g - 1)
                    turn(1, 1 - u)
                    pe.wait_ge(sem("part_hi0"), g)
                    pe.matmul(ps[:, TURN_BANK[0], :], minus[:, :], probsT_hi[:, 1 - u, 0, :], start=False, stop=True,
                              skip_group_check=True).then_inc(sem("head_taken"), 1)
                if old:
                    weigh(1)
                    weigh(2)
                    weigh(3).then_inc(sem("weighed"), 1)

            attention(0, LAYER1, pe, step)
            def turn_z(k, u):
                pe.wait_ge(sem(f"z_in{u}"), (k - u) * 8 + 16)
                since(pe, sem("p2_zT_a"), k - 1)
                since(pe, sem("p2_zT_b"), k - 1)
                for c in range(H * G):
                    last = pe.transpose(banks16(2 * u, 2)[:, c * P:(c + 1) * P], z_in(u)[:, c * P:(c + 1) * P], ident_h[:, :])
                last.then_inc(sem("p2_zT"), 1)

            def turn_h2(k, u):
                pe.wait_ge(sem("p2_lo"), k + 1)
                since(pe, sem("p2_hT"), k - 1)
                for s in range(G):
                    last = pe.transpose(banks16(6 + u, 1)[:, s * P:(s + 1) * P], h_parts(u)[:, s * P:(s + 1) * P], ident_h[:, :])
                last.then_inc(sem("p2_turned"), 1)

            def p2_step(k, u):
                pe.wait_ge(sem("p2_zT_a"), k + 1)
                pe.wait_ge(sem("p2_zT_b"), k + 1)
                since(pe, sem("p2_lo"), k - 1)
                for s in range(G):
                    for h in range(H):
                        for part in range(2):
                            last = pe.matmul(ps[:, 4 + u, s * D:(s + 1) * D], zT_parts(u)[:, (h * G + s) * P:(h * G + s + 1) * P],
                                             w16[:, 1, part, h * D:(h + 1) * D],
                                             start=(h == 0 and part == 0), stop=(h == H - 1 and part == 1))
                last.then_inc(sem("p2_h"), 1)
                if within(k + 1):
                    turn_z(k + 1, 1 - u)
                if within(k - 1):
                    turn_h2(k - 1, 1 - u)

            turn_z(0, 0)
            units(pe, p2_step)
            turn_h2(UNITS - 1, 1)
            attention(LAYER1, INSTANCES, pe, step)

        @block.scalar
        def _(act):
            act.wait_ge(sem("a_turned"), 4)
            for q in range(4):
                act.copy(aT[:, 4 * q:4 * q + 4, :], ps[:, 2 + q, :].rearrange("p (j n) -> p j n", j=4)).then_inc(sem("a_copied"), 1)
            with strided(act, 0, NT, 2) as t:
                for u in range(2):
                    act.wait_ge(sem("xT"), t + u + 1)
                    act.wait_ge(sem("h_ready"), t + u)
                    act.copy(work2[:, u, :], ps[:, 4 + u, :]).then_inc(sem("xT_copied"), 1)
                    act.wait_ge(sem("h32"), t + u + 1)
                    act.activation(h_hi[:, bass.ts(t + u, BD)], h32[:, u * BD:(u + 1) * BD], ACT.Copy,
                                   scale=node_on[:, bass.ds(t + u, 1)]).then_inc(sem("hi_made"), 1)
            act.wait_ge(sem("hsum_ready"), 1)
            act.copy(hsum[:, :], ps[:, 4, :]).then_inc(sem("hsum_copied"), 1)
            with act.Fori(0, NT) as i:
                act.wait_ge(sem("a_centred"), i + 1)
                act.square(work[:, 3, :], work[:, 2, :]).then_inc(sem("a_squared"), 1)
            def copy_xT(k, u):
                act.wait_ge(sem("p1_xT"), k + 1)
                since(act, sem("p1_h"), k - 1)
                act.copy(xT_parts(u), banks16(u, 1)[:, 0:G * P]).then_inc(sem("p1_xT_copied"), 1)

            def copy_hT(k, u):
                act.wait_ge(sem("p1_hT"), k + 1)
                since(act, sem(f"hT_stored{u}"), stores(k, u))
                act.copy(hT_parts(u)[:, 0:2 * G * P], banks16(6, 1)).then_inc(sem("p1_hT_a"), 1)

            def p1_step(k, u):
                act.wait_ge(sem("p1_h"), k + 1)
                since(act, sem("p1_hT"), k - 1)
                since(act, sem(f"h_stored{u}"), stores(k, u))
                act.copy(by_tiles(h_parts(u), 0), products(u)).then_inc(sem("p1_hi"), 1)
                if within(k + 1):
                    copy_xT(k + 1, 1 - u)
                if within(k - 1):
                    copy_hT(k - 1, 1 - u)

            copy_xT(0, 0)
            units(act, p1_step)
            copy_hT(UNITS - 1, 1)

            def step(g, u, instance, t, parity, tile):
                if tile(1):
                    old, tt = tile(1)
                    act.wait_ge(sem("masked1"), g)
                    since(act, sem("turned3"), g - 2)
                    act.activation(probs[:, 1 - u, :], scores[:, 1 - u, :], ACT.Exp, bias=neg_max[:, 1 - u:2 - u], scale=-1.0,
                                   accum_out=col(row_sum[:, old], tt)).then_inc(sem("exp_done"), 1)
                def head(q, slot, n):
                    act.wait_ge(sem(f"turned{q}"), n)
                    act.activation(probsT_hi[:, slot, q, :], ps[:, TURN_BANK[q], :], ACT.Copy, scale=SCALE).then_inc(sem(f"part_hi{q}"), 1)

                if tile(2):
                    head(3, u, g - 1)
                if tile(1):
                    head(0, 1 - u, g)
                    head(2, 1 - u, g)
                    head(1, 1 - u, g)
                    act.wait_ge(sem("head_taken"), g)
                    act.activation(probsT_lo[:, 1 - u, 0, :], ps[:, TURN_BANK[0], :], ACT.Copy, scale=SCALE).then_inc(sem("part_lo0"), 1)

            attention(0, LAYER1, act, step)
            def copy_zT(k, u):
                act.wait_ge(sem("p2_zT"), k + 1)
                since(act, sem("p2_h"), k - 1)
                act.copy(zT_parts(u)[:, 0:2 * G * P], banks16(2 * u, 1)).then_inc(sem("p2_zT_a"), 1)

            def p2_step(k, u):
                act.wait_ge(sem("p2_h"), k + 1)
                since(act, sem("p2_turned"), k - 1)
                since(act, sem(f"h2_stored{u}"), stores(k, u))
                act.copy(tile_part(u, 0), ps[:, 4 + u, 0:G * D].rearrange("p (s d) -> p s d", s=G)).then_inc(sem("p2_hi"), 1)
                if within(k + 1):
                    copy_zT(k + 1, 1 - u)
                if within(k - 1):
                    copy_h2T(k - 1, 1 - u)

            def copy_h2T(k, u):
                act.wait_ge(sem("p2_turned"), k + 1)
                since(act, sem(f"h2T_stored{u}"), stores(k, u))
                act.copy(hT_parts(u)[:, 0:G * P], banks16(6 + u, 1)[:, 0:G * P]).then_inc(sem("p2_hT"), 1)

            copy_zT(0, 0)
            units(act, p2_step)
            copy_h2T(UNITS - 1, 1)
            attention(LAYER1, INSTANCES, act, step)

        @block.vector
        def _(dve):
            dve.sem_inc(sem("neigh_free"), 8)
            dve.wait_ge(sem("weights_loaded"), 16 * 9)
            dve.memset(ones16, 1.0).then_inc(sem("ones_made"), 1)
            dve.wait_ge(sem("weights_turned"), 1)
            dve.wait_ge(sem("w0T2_cleared"), 1)
            for k in range(2):
                dve.tensor_copy(w0T2[k * D:(k + 1) * D, k * D:(k + 1) * D], ps[0:D, 0, 0:D]).then_inc(sem("weights_copied"), 1)
            for k, wT in enumerate((ps[0:D, 0, D:D + H * D], ps[0:D, 1, 0:H * D])):
                for half in range(2):
                    w = slice(half * D, (half + 1) * D)
                    dve.tensor_copy(w16[w, k, 0, :], wT).then_inc(sem("w16_hi"), 1)
                dve.wait_ge(sem("w16_hi"), 2 * k + 2)
                for half in range(2):
                    w = slice(half * D, (half + 1) * D)
                    dve.tensor_tensor(w16[w, k, 1, :], wT, w16[0:D, k, 0, :], ALU.subtract).then_inc(sem("w16_lo"), 1)
            dve.wait_ge(sem("a_copied"), 4)
            b0_all = rows[:, 0:1, :].to_broadcast([P, B, D])
            with strided(dve, 0, NT, 2) as t:
                for u in range(2):
                    dve.wait_ge(sem("h_ready"), t + u + 1)
                    hv = pair(h32[:, u * BD:(u + 1) * BD])
                    dve.tensor_tensor(hv, pair(ps[:, 6 + u, :]), b0_all, ALU.add).then_inc(sem("h32"), 1)
                    dve.wait_ge(sem("h32"), t + u + 1)
                    prod = pair(h32[:, 2 * BD:3 * BD])
                    dve.tensor_tensor(prod, hv, aT[:, bass.ds(t + u, 1), 0:D].to_broadcast([P, B, D]), ALU.mult).then_inc(sem("s1_prod"), 1)
                    dve.wait_ge(sem("s1_prod"), t + u + 1)
                    dve.tensor_reduce(s1[:, t + u, :], prod, AX.X, ALU.add).then_inc(sem("s1_made"), 1)
                    dve.wait_ge(sem("s1_made"), t + u + 1)
                    dve.wait_ge(sem("hi_made"), t + u + 1)
                    dve.scalar_tensor_tensor(h_lo[:, bass.ts(t + u, BD)], h32[:, u * BD:(u + 1) * BD], node_on[:, bass.ds(t + u, 1)],
                                             h_hi[:, bass.ts(t + u, BD)], ALU.mult, ALU.subtract).then_inc(sem("lo_made"), 1)
                    dve.wait_ge(sem(f"adj_loaded{u}"), t * 8 + 16)
                    dve.tensor_scalar(mask[:, bass.ts(t + u, N)].rearrange("p (t q) -> p t q", t=NT),
                                      adj_slot[:, u, :].rearrange("p (q t) -> p t q", t=NT), 0.0, None, ALU.is_gt).then_inc(sem("mask_made"), 1)
            dve.wait_ge(sem("hsum_copied"), 1)
            with strided(dve, 0, NT, 8) as i0:
                for j in range(8):
                    i = i0 + j
                    if j % 4 == 0:
                        dve.wait_ge(sem("neigh_ready"), i0 // 4 + j // 4 + 1)
                    prod = pair(work[:, 0, :])
                    dve.tensor_tensor(prod, pair(ps[:, j, :]), aT[:, bass.ds(i, 1), D:P].to_broadcast([P, B, D]), ALU.mult).then_inc(sem("neigh_free"), 1)
                    dve.wait_ge(sem("neigh_free"), i + 9)
                    dve.tensor_reduce(small[:, 0, 0:B], prod, AX.X, ALU.add).then_inc(sem("s2_made"), 1)
                    dve.wait_ge(sem("s2_made"), i + 1)
                    dve.tensor_tensor(small[:, 1, 0:B], small[:, 0, 0:B], s1[:, i, :], ALU.add).then_inc(sem("s_sum"), 1)
                    dve.wait_ge(sem("s_sum"), i + 1)
                    dve.tensor_scalar(small[:, 1, 0:B], small[:, 1, 0:B], node_on[:, bass.ds(i, 1)], None, ALU.mult).then_inc(sem("s_made"), 1)
                    dve.wait_ge(sem("s_made"), i + 1)
                    y, c = pair(work[:, 1, :]), pair(work[:, 2, :])
                    dve.tensor_tensor(prod, pair(hsum[:, :]), small[:, 1, 0:B].rearrange("p (b o) -> p b o", o=1).to_broadcast([P, B, D]), ALU.mult).then_inc(sem("hp"), 1)
                    dve.wait_ge(sem("hp"), i + 1)
                    dve.scalar_tensor_tensor(work[:, 1, :], work[:, 0, :], 0.01, work[:, 0, :], ALU.mult, ALU.max).then_inc(sem("hp_leaky"), 1)
                    dve.wait_ge(sem("hp_leaky"), i + 1)
                    dve.tensor_tensor(y, y, x_btc[:, :, i, :], ALU.add).then_inc(sem("a_y"), 1)
                    dve.wait_ge(sem("a_y"), i + 1)
                    dve.tensor_reduce(small[:, 0, 0:B], y, AX.X, ALU.add).then_inc(sem("a_mean"), 1)
                    dve.wait_ge(sem("a_mean"), i + 1)
                    dve.scalar_tensor_tensor(c, small[:, 0, 0:B].rearrange("p (b o) -> p b o", o=1).to_broadcast([P, B, D]), -1.0 / D, y,
                                             ALU.mult, ALU.add).then_inc(sem("a_centred"), 1)
                    dve.wait_ge(sem("a_squared"), i + 1)
                    dve.tensor_reduce(small[:, 2, 0:B], pair(work[:, 3, :]), AX.X, ALU.add).then_inc(sem("a_ssq"), 1)
                    dve.wait_ge(sem("a_ssq"), i + 1)
                    dve.tensor_scalar(small[:, 2, 0:B], small[:, 2, 0:B], 1.0 / D, EPS, ALU.mult, ALU.add).then_inc(sem("a_var"), 1)
                    dve.wait_ge(sem("a_rstd"), i + 1)
                    dve.wait_ge(sem("a_centred"), i + 1)
                    dve.tensor_tensor(x_btc[:, :, i, :], c, small[:, 3, 0:B].rearrange("p (b o) -> p b o", o=1).to_broadcast([P, B, D]),
                                      ALU.mult).then_inc(sem("x1_done"), 1)
            with dve.Fori(0, NT) as t:
                d = mask[:, bass.ds(t * (N + P), P)]
                dve.tensor_tensor(d, d, ident16[:, :], ALU.max).then_inc(sem("mask_diag"), 1)
                dve.wait_ge(sem("mask_diag"), t + 1)
                m = mask[:, bass.ts(t, N)]
                dve.tensor_scalar(m, m, -1.0, MASKED_SCORE, ALU.add, ALU.mult).then_inc(sem("mask_ready"), 1)
            def copy_hT(k, u):
                dve.wait_ge(sem("p1_hT"), k + 1)
                since(dve, sem(f"hT_stored{u}"), stores(k, u))
                dve.tensor_copy(hT_parts(u)[:, 2 * G * P:4 * G * P], banks16(7, 1)).then_inc(sem("p1_hT_b"), 1)

            def p1_step(k, u):
                dve.wait_ge(sem("p1_hi"), k + 1)
                dve.tensor_tensor(by_tiles(h_parts(u), 1), products(u), by_tiles(h_parts(u), 0), ALU.subtract).then_inc(sem("p1_lo"), 1)
                if within(k - 1):
                    copy_hT(k - 1, 1 - u)

            units(dve, p1_step)
            copy_hT(UNITS - 1, 1)

            def step(g, u, instance, t, parity, tile):
                def masked(c):
                    dve.wait_ge(sem(f"scores{c}"), g + 1)
                    if c == 1:
                        dve.wait_ge(sem("masked0"), g + 1)
                    w = slice(c * 2 * BANK, (c + 1) * 2 * BANK)
                    if c == 0:
                        dve.wait_ge(sem(f"mask_staged{u}"), (g - u) * 8 + 16)
                        since(dve, sem("exp_done"), g - 1)
                    gate(dve, "dve")
                    start = 3.0e38 if c == 0 else neg_max0[:, u:u + 1]
                    dve.tensor_tensor_reduce(scores[:, u, w], ps[:, 2 * c:2 * c + 2, :].rearrange("p a n -> p (a n)"), mask_slot[:, u, w],
                                             -1.0, start, ALU.add, ALU.min,
                                             (neg_max0 if c == 0 else neg_max)[:, u:u + 1]).then_inc(sem(f"masked{c}"), 1)

                def remainder(q, slot, n):
                    dve.wait_ge(sem(f"part_hi{q}"), n)
                    dve.scalar_tensor_tensor(probsT_lo[:, slot, q, :], ps[:, TURN_BANK[q], :], SCALE, probsT_hi[:, slot, q, :],
                                             ALU.mult, ALU.subtract).then_inc(sem(f"part_lo{q}"), 1)

                if t is not None:
                    masked(0)
                if tile(2):
                    remainder(3, u, g - 1)
                if t is not None:
                    masked(1)
                if tile(1):
                    remainder(2, 1 - u, g)
                    remainder(1, 1 - u, g)
                if isinstance(t, int) and t == 1:
                    outs_free(instance, parity)
                if tile(2):
                    old, tt = tile(2)
                    dve.wait_ge(sem("inverse"), g - 1)
                    dve.wait_ge(sem("weighed"), g - 1)
                    dve.tensor_scalar(col(outs[:, old], tt, D), ps[:, 7, 0:D], row_inv[:, u:u + 1], 1.0 / SCALE,
                                      ALU.mult, ALU.mult).then_inc(sem("normed"), 1)
                if tile(1):
                    new, tt = tile(1)
                    dve.wait_ge(sem("exp_done"), g)
                    dve.reciprocal(row_inv[:, 1 - u:2 - u], col(row_sum[:, new], tt)).then_inc(sem("inverse"), 1)

            def outs_free(instance, parity):
                since(dve, sem("z_lo"), instance - 1)

            attention(0, LAYER1, dve, step)
            def copy_zT(k, u):
                dve.wait_ge(sem("p2_zT"), k + 1)
                since(dve, sem("p2_h"), k - 1)
                dve.tensor_copy(zT_parts(u)[:, 2 * G * P:4 * G * P], banks16(2 * u + 1, 1)).then_inc(sem("p2_zT_b"), 1)

            def p2_step(k, u):
                dve.wait_ge(sem("p2_hi"), k + 1)
                dve.tensor_tensor(tile_part(u, 1), ps[:, 4 + u, 0:G * D].rearrange("p (s d) -> p s d", s=G), tile_part(u, 0),
                                  ALU.subtract).then_inc(sem("p2_lo"), 1)
                if within(k + 1):
                    copy_zT(k + 1, 1 - u)

            copy_zT(0, 0)
            units(dve, p2_step)

            def outs_free(instance, parity):
                if isinstance(instance, int) and instance < LAYER1 + 2:
                    dve.wait_ge(sem("z_lo"), LAYER1)
                else:
                    dve.wait_ge(sem("f_residual"), (instance - (LAYER1 + 1)) * 2)

            attention(LAYER1, INSTANCES, dve, step)
            dve.wait_ge(sem("normed"), INSTANCES * NT)
            dve.wait_ge(sem("f_done"), 2 * B - 1)
            finish(dve, 2 * B - 1, outs[:, 1, HALF:2 * HALF], "last")


_INS = ['x', 'adj', 'L0_gnn_W_w', 'L0_gnn_W_b', 'L0_gnn_a', 'L1_gnn_Wh', 'L1_gnn_bh', 'L1_gnn_Wo', 'L1_gnn_bo',
        'L1_gnn_gamma', 'L1_gnn_beta']


def kernel(**inputs):
    import numpy as _np
    import concourse.bacc as _bacc
    from concourse import mybir as _mybir
    from concourse.bass_utils import run_bass_kernel_spmd as _run

    nc = _bacc.Bacc("TRN2", target_bir_lowering=False, num_devices=1)
    arrays, args = {}, []
    for name in _INS:
        v = _np.ascontiguousarray(inputs[name])
        arrays[f"in_{name}"] = v
        args.append(nc.dram_tensor(f"in_{name}", v.shape, _mybir.dt.from_np(v.dtype), kind="ExternalInput").ap())
    args.append(nc.dram_tensor("out_0", (B, N, D), F32, kind="ExternalOutput").ap())
    build(nc, *args)
    r = _run(nc, [arrays], core_ids=[0])
    return r.results[0]["out_0"]
```

```python
from contextlib import ExitStack, contextmanager

import concourse.bass as bass
from concourse import mybir

ALU = mybir.AluOpType
ACT = mybir.ActivationFunctionType
AX = mybir.AxisListType
F32 = mybir.dt.float32
F16 = mybir.dt.float16
BF16 = mybir.dt.bfloat16
I32 = mybir.dt.int32
U32 = mybir.dt.uint32

P = 128
B, N, D = 8, 2048, 64
H = 4
NT = N // P
BD = B * D
BANK = 512
SCALE = 32768.0
MASKED_SCORE = 1e16
EPS = 1e-5
LAYER1 = B * H
INSTANCES = LAYER1 + B
OPERAND_DMAS = 6
G = 4
UNITS = B * NT // G
FINISH_STEPS = 42
HALF = NT // 2 * D


def build(nc, x, adj, w0, b0, a, wh, bh, wo, bo, gamma, beta, out):
    ctx = ExitStack()
    with ctx:
        def sb(name, shape, dt):
            return ctx.enter_context(nc.sbuf_tensor(name, shape, dt))

        def dram(name, shape, dt):
            return nc.dram_tensor(name, shape, dt, kind="Internal").ap()

        made = {}

        def sem(name):
            if name not in made:
                made[name] = ctx.enter_context(nc.semaphore(name))
            return made[name]

        hT_d = dram("hT_d", [INSTANCES * P, N], F16)
        h_d = dram("h_d", [P, INSTANCES, NT * P], F16)
        z_d = dram("z_d", [P, LAYER1, NT * P], F16)

        mask = sb("mask", [P, NT * N], BF16)
        xs = sb("xs", [P, B * NT * D], F32)
        x_btc = xs[:, :].rearrange("p (b t c) -> p b t c", b=B, t=NT)
        ident = sb("ident", [P, P], F32)
        ident16 = sb("ident16", [P, P], BF16)
        ident_h = sb("ident_h", [P, P], F16)
        node_on = sb("node_on", [P, NT], F32)
        w0T2 = sb("w0T2", [P, P], F32)
        w16 = sb("w16", [P, 2, 2, H * D], F16)
        bh_rows = sb("bh_rows", [P, H, D], F32)
        rows = sb("rows", [P, 4, D], F32)
        hsum = sb("hsum", [P, BD], F32)
        s1 = sb("s1", [P, NT, B], F32)
        half_neg = sb("half_neg", [P, NT], F32)
        operands = sb("operands", [P, 3, 2, N], F16)
        q_head = operands[:, 0]
        q_tail = operands[:, 1]
        k_both = operands[:, 2]
        v_parts = sb("v_parts", [P, 2, NT * P], F16)
        scores = sb("scores", [P, 2, N], F32)
        probs = sb("probs", [P, 2, N], F32)
        probsT = sb("probsT", [P, 2, 2, 4, BANK], F16)
        probsT_hi, probsT_lo = probsT[:, 0], probsT[:, 1]
        mask_slot = sb("mask_slot", [P, 2, N], BF16)
        outs = sb("outs", [P, 2, NT * D], F32)
        scratch = sb("scratch", [P, NT * D], F32)
        z_parts = scratch[:, :].bitcast(F16)
        neg_max0 = sb("neg_max0", [P, 2], F32)
        neg_max = sb("neg_max", [P, 2], F32)
        row_sum = sb("row_sum", [P, 2, NT], F32)
        row_inv = sb("row_inv", [P, 2, NT], F32)
        adj_slot = scores[:, :, :].bitcast(I32)
        h_hi = probs[:, :, :].rearrange("p u n -> p (u n)").bitcast(F16)
        h_lo = operands[:, 0:2].rearrange("p a u n -> p (a u n)")
        shifted = k_both[:, 0, 0:2 * BD]
        a_in = v_parts[:, :, :].rearrange("p u n -> p (u n)").bitcast(F32)
        work = probsT[:, 0].rearrange("p a k n -> p (a k n)").bitcast(F32).rearrange("p (k n) -> p k n", k=4)
        work2 = outs[:, :, :].rearrange("p u n -> p (u n)").rearrange("p (k n) -> p k n", k=4)
        h32 = mask_slot[:, :, :].rearrange("p u n -> p (u n)").bitcast(F32)
        aT = probsT[:, 1].rearrange("p a k n -> p (a k n)").bitcast(F32).rearrange("p (t f) -> p t f", t=NT)
        a_work = (work, h32.rearrange("p (k n) -> p k n", k=4))
        w_nat = scratch[:, 0:7 * D]
        small = sb("small", [P, 4, NT], F32)
        stats = sb("stats", [P, 3, NT // 2], F32)

        ps = ctx.enter_context(nc.psum_tensor("ps", [P, 8, BANK], F32))

        block = ctx.enter_context(nc.Block())

        def pair(ap):
            return ap.rearrange("p (b c) -> p b c", c=D)

        def attention(first, last, eng, step, peeled=2):
            def apart(instance, parity, tiles, fresh):
                for t in tiles:
                    def tile(lag, t=t):
                        if t >= lag:
                            return parity, t - lag
                        return None if fresh else (1 - parity, NT + t - lag)
                    step(instance * NT + t, t % 2, instance, t, parity, tile)

            def head(instance, parity, fresh=False):
                apart(instance, parity, range(2), fresh)

            def body(instance, parity, fresh=False):
                apart(instance, parity, range(2, peeled), fresh)
                with strided(eng, peeled, NT, 2) as t:
                    for u in range(2):
                        step(instance * NT + t + u, u, instance, t + u, parity, lambda lag: (parity, t + u - lag))

            head(first, 0, True)
            body(first, 0, True)
            head(first + 1, 1)
            with strided(eng, first, last - 2, 2) as i:
                for k in range(2):
                    body(i + k + 1, 1 - k)
                    head(i + k + 2, k)
            body(last - 1, 1)
            for t in range(NT, NT + 3):
                step((last - 1) * NT + t, t % 2, last - 1, None, 1, lambda lag: (1, t - lag) if t - lag < NT else None)

        @contextmanager
        def strided(eng, first, end, by):
            with eng.Fori(first // by, end // by) as i:
                yield i * by

        def col(ap, i, w=1):
            return ap[:, i * w:(i + 1) * w] if isinstance(i, int) else ap[:, bass.ts(i, w)]

        def gate(eng, name):
            eng.sem_inc(sem(f"{name}_gate"), 1)

        def since(eng, s, n):
            if not (isinstance(n, int) and n <= 0):
                eng.wait_ge(s, n)

        def stage16(buffer, u, at, n):
            return buffer[:, u, at // 2:(at + n) // 2].bitcast(F16)

        def x_parts(u):
            return stage16(scores, u, 0, G * P).rearrange("p (s k c) -> p s k c", s=G, k=2)

        def xT_parts(u):
            return stage16(scores, u, G * P, G * P)

        def z_in(u):
            return stage16(scores, u, 0, H * G * P)

        def zT_parts(u):
            return stage16(scores, u, H * G * P // 2 * 2, H * G * P)

        def h_parts(u):
            return stage16(probs, u, 0, H * G * P)

        def hT_parts(u):
            return stage16(probs, u, H * G * P, H * G * P)

        def banks16(bank, n):
            return ps[:, bank:bank + n, :].rearrange("p a n -> p (a n)").bitcast(F16)

        def outs_free(eng, instance):
            since(eng, sem("outs_taken"), instance - 1)

        def units(eng, step):
            step(0, 0)
            step(1, 1)
            with strided(eng, 2, UNITS - 2, 2) as k:
                for u in range(2):
                    step(k + u, u)
            step(UNITS - 2, 0)
            step(UNITS - 1, 1)

        def within(k):
            return not isinstance(k, int) or 0 <= k < UNITS

        ones16 = k_both[:, 1, 0:P]
        TURN_BANK = (4, 5, 6, 5)

        def products(u):
            return ps[:, 2 + 2 * u:4 + 2 * u, :].rearrange("p a n -> p (a n)").rearrange("p (s h d) -> p s h d", s=G, h=H)

        def by_tiles(parts, part):
            return parts.rearrange("p (h s k d) -> p s h k d", h=H, s=G, k=2)[:, :, :, part, :]

        def tile_part(u, part):
            return h_parts(u)[:, 0:G * P].rearrange("p (s k d) -> p s k d", s=G, k=2)[:, :, part, :]

        def stores(k, u):
            return (k - u) * 8

        def half_x1(c):
            return col(xs, c, HALF)

        def half_out(b, half):
            return out[b].rearrange("(p t) c -> p (t c)", t=NT)[:, half * HALF:(half + 1) * HALF]

        def finish(eng, c, u, half, name):
            last = name == "last"
            n = 1 if last else c + 1
            x1 = half_x1(c)
            y = outs[:, u, half * HALF:(half + 1) * HALF]
            inverses = row_inv[:, u, half * (NT // 2):(half + 1) * (NT // 2)]
            squares = scratch[:, 0:HALF]

            def grid(ap):
                return ap.rearrange("p (t c) -> p t c", c=D)

            def over_features(ap):
                return ap.rearrange("p (t o) -> p t o", o=1).to_broadcast([P, NT // 2, D])

            def row(k):
                return rows[:, k:k + 1, :].to_broadcast([P, NT // 2, D])

            steps = []

            def then(instruction):
                steps.append(1)
                instruction.then_inc(sem(f"{name}_step"), 1)
                eng.wait_ge(sem(f"{name}_step"), len(steps) if last else c * FINISH_STEPS + len(steps))
                gate(eng, name)

            def signal(what, instruction, n):
                instruction.then_inc(sem(f"{name}_{what}"), 1)
                eng.wait_ge(sem(f"{name}_{what}"), n)
                gate(eng, name)

            def total(v, k):
                if last:
                    then(eng.tensor_reduce(stats[:, k, :], grid(v), AX.X, ALU.add))
                    return
                w, v, s = D // 2, grid(v), grid(squares)
                while w:
                    o = s[:, :, 0:w] if w > 1 else stats[:, k, :].rearrange("p (t o) -> p t o", o=1)
                    then(eng.tensor_tensor(o, v[:, :, 0:w], v[:, :, w:2 * w], ALU.add))
                    v, w = s, w // 2

            def centred(v, k):
                total(v, 0)
                then(eng.tensor_scalar(stats[:, 0, :], stats[:, 0, :], -1.0 / D, 0.0, ALU.mult, ALU.add))
                then(eng.tensor_tensor(grid(v), grid(v), over_features(stats[:, 0, :]), ALU.add))
                then(eng.tensor_tensor(squares, v, v, ALU.mult))
                total(squares, 1)
                var = eng.tensor_scalar(stats[:, 1, :], stats[:, 1, :], 1.0 / D, EPS, ALU.mult, ALU.add)
                if last:
                    signal("var", var, k + 1)
                    eng.wait_ge(sem("last_rstd"), k + 1)
                else:
                    then(var)
                    then(eng.tensor_tensor(stats[:, 2, :], stats[:, 1, :], half_neg[:, 0:NT // 2], ALU.pow))

            then(eng.tensor_tensor(grid(y), grid(y), over_features(inverses), ALU.mult))
            then(eng.tensor_tensor(grid(y), grid(y), row(1), ALU.add))
            then(eng.tensor_scalar(squares, y, 0.0, -0.8, ALU.min, ALU.mult))
            then(eng.tensor_tensor(y, y, squares, ALU.add))
            centred(y, 0)
            then(eng.tensor_tensor(grid(y), grid(y), over_features(stats[:, 2, :]), ALU.mult))
            then(eng.tensor_tensor(grid(y), grid(y), row(2), ALU.mult))
            then(eng.tensor_tensor(grid(y), grid(y), row(3), ALU.add))
            then(eng.tensor_tensor(x1, x1, y, ALU.add))
            if half == 1 and not last:
                eng.sem_inc(sem("outs_taken"), 1)
            centred(x1, 1)
            signal("done", eng.tensor_tensor(grid(x1), grid(x1), over_features(stats[:, 2, :]), ALU.mult), n)
            assert last or len(steps) == FINISH_STEPS

        @block.sync
        def _(sp):
            for b in range(B):
                sp.dma_start(xs[:, b * NT * D:(b + 1) * NT * D],
                             x[b].rearrange("(p t) c -> p (t c)", t=NT)).then_inc(sem("x_loaded"), 16)
            sp.dma_start(w_nat[0:D, 0:D], w0).then_inc(sem("weights_loaded"), 16)
            sp.dma_start(w_nat[:, D:3 * D].rearrange("p (k c) -> p k c", k=2),
                         wh.rearrange("(k h) d c -> (h d) k c", k=2)).then_inc(sem("weights_loaded"), 16)
            sp.dma_start(w_nat[0:D, 3 * D:7 * D], wo).then_inc(sem("weights_loaded"), 16)
            sp.dma_start(bh_rows[:, :, :].rearrange("p h d -> p (h d)"),
                         bh.rearrange("h d -> (h d)").rearrange("(o n) -> o n", o=1).to_broadcast([P, H * D])).then_inc(sem("weights_loaded"), 16)
            sp.dma_start(a_in, a).then_inc(sem("weights_loaded"), 16)
            for k, row in enumerate((b0, bo, gamma, beta)):
                sp.dma_start(rows[:, k, :], row.rearrange("(o c) -> o c", o=1).to_broadcast([P, D])).then_inc(sem("weights_loaded"), 16)
            def load_adj(t, u):
                sp.dma_start(adj_slot[:, u, :],
                             adj.rearrange("(p t) m -> p (t m)", t=NT)[:, bass.ts(t, N)]).then_inc(sem(f"adj_loaded{u}"), 16)

            load_adj(0, 0)
            load_adj(1, 1)
            with strided(sp, 2, NT, 2) as t:
                for u in range(2):
                    sp.wait_ge(sem("mask_made"), t + u - 1)
                    load_adj(t + u, u)
            sp.wait_ge(sem("lo_made"), NT)
            sp.wait_ge(sem("shift_cleared"), 1)
            sp.wait_ge(sem("hi_made"), NT)
            for lo, hi in ((0, 112), (112, 127)):
                sp.dma_start(shifted[lo + 1:hi + 1, 0:BD], h_hi[lo:hi, (NT - 1) * BD:NT * BD]).then_inc(sem("shifted_in"), 16)
                sp.dma_start(shifted[lo + 1:hi + 1, BD:2 * BD], h_lo[lo:hi, (NT - 1) * BD:NT * BD]).then_inc(sem("shifted_in"), 16)

            with sp.Fori(0, B) as b:
                for j in range(NT // G):
                    u = j % 2
                    k = b * (NT // G) + j
                    sp.wait_ge(sem("p1_lo"), k + 1)
                    sp.dma_start(h_d[:, bass.ts(b, H), j * G * P:(j + 1) * G * P],
                                 h_parts(u).rearrange("p (h n) -> p h n", h=H)).then_inc(sem(f"h_stored{u}"), 16)
                    sp.wait_ge(sem("p1_hT_a"), k + 1)
                    sp.wait_ge(sem("p1_hT_b"), k + 1)
                    sp.dma_start(hT_d[bass.ts(b, H * P), j * G * P:(j + 1) * G * P].rearrange("(h q) n -> q h n", h=H),
                                 hT_parts(u).rearrange("p (h n) -> p h n", h=H)).then_inc(sem(f"hT_stored{u}"), 16)
            for u in range(2):
                sp.wait_ge(sem(f"h_stored{u}"), 8 * UNITS)
                sp.wait_ge(sem(f"hT_stored{u}"), 8 * UNITS)

            def load_part(i, parity, k):
                s = sem(f"operands{parity}")
                if k == 5:
                    sp.dma_start(v_parts[:, parity, :], h_d[:, i, :] if isinstance(i, int) else h_d[:, bass.ds(i, 1), :]).then_inc(s, 16)
                    return
                to, half, part, rows_ = ((q_head, 0, 0, D), (q_tail, 0, 1, D), (k_both, 0, 0, P), (q_head, 1, 0, D), (q_tail, 1, 1, D))[k]
                at = i * P + part * D
                sp.dma_start(to[half * D:half * D + rows_, parity, :],
                             hT_d[at:at + rows_, :] if isinstance(i, int) else hT_d[bass.ds(at, rows_), :]).then_inc(s, 16)

            for i in range(2):
                for k in range(OPERAND_DMAS):
                    load_part(i, i, k)

            def step(g, u, instance, t, parity, tile):
                if t is None:
                    return
                if not (isinstance(g, int) and g == 0):
                    sp.wait_ge(sem("masked1"), g)
                    gate(sp, "sp")
                sp.dma_start(mask_slot[:, 1 - u, :], col(mask, (t + 1) % NT, N)).then_inc(sem(f"mask_staged{1 - u}"), 16)
                k = t - 2 if isinstance(t, int) else OPERAND_DMAS
                if 0 <= k < OPERAND_DMAS and more(instance):
                    if k == 0:
                        sp.wait_ge(sem("weighed"), instance * NT)
                        gate(sp, "sp")
                    load_part(instance + 1, 1 - parity, k)

            def more(instance):
                return not isinstance(instance, int) or instance not in (0, LAYER1 - 1, LAYER1, INSTANCES - 1)

            sp.wait_ge(sem("mask_ready"), NT)
            sp.dma_start(mask_slot[:, 0, :], mask[:, 0:N]).then_inc(sem("mask_staged0"), 16)
            attention(0, LAYER1, sp, step, 2 + OPERAND_DMAS)
            sp.wait_ge(sem("z_stored"), 16 * LAYER1)

            def load_z(b, j):
                sp.dma_start(z_in(j % 2).rearrange("p (h n) -> p h n", h=H),
                             z_d[:, b * H:(b + 1) * H, j * G * P:(j + 1) * G * P] if isinstance(b, int) else
                             z_d[:, bass.ts(b, H), j * G * P:(j + 1) * G * P]).then_inc(sem(f"z_in{j % 2}"), 16)

            load_z(0, 0)
            load_z(0, 1)

            def serve_units(b, last):
                for j in range(NT // G):
                    u = j % 2
                    k = b * (NT // G) + j
                    if not (last and j >= 2):
                        sp.wait_ge(sem("p2_zT"), k + 1)
                        load_z(b + j // 2, (j + 2) % (NT // G))
                    sp.wait_ge(sem("p2_lo"), k + 1)
                    sp.dma_start(h_d[:, LAYER1 + b, j * G * P:(j + 1) * G * P] if isinstance(b, int) else
                                 h_d[:, bass.ds(b + LAYER1, 1), j * G * P:(j + 1) * G * P],
                                 h_parts(u)[:, 0:G * P]).then_inc(sem(f"h2_stored{u}"), 16)
                    sp.wait_ge(sem("p2_hT"), k + 1)
                    sp.dma_start(hT_d[(LAYER1 + b) * P:(LAYER1 + b + 1) * P, j * G * P:(j + 1) * G * P] if isinstance(b, int) else
                                 hT_d[bass.ts(b + LAYER1, P), j * G * P:(j + 1) * G * P],
                                 hT_parts(u)[:, 0:G * P]).then_inc(sem(f"h2T_stored{u}"), 16)

            with sp.Fori(0, B - 1) as b:
                serve_units(b, False)
            serve_units(B - 1, True)
            for u in range(2):
                sp.wait_ge(sem(f"h2_stored{u}"), 8 * UNITS)
                sp.wait_ge(sem(f"h2T_stored{u}"), 8 * UNITS)
            for i in range(2):
                for k in range(OPERAND_DMAS):
                    load_part(LAYER1 + i, i, k)

            attention(LAYER1, INSTANCES, sp, step, 2 + OPERAND_DMAS)
            sp.wait_ge(sem("mask_staged0"), 16 * (INSTANCES * NT // 2 + 1))
            sp.wait_ge(sem("last_done"), 1)
            sp.dma_start(half_out(B - 1, 1), half_x1(2 * B - 1)).then_inc(sem("last_stored"), 16)
            sp.wait_ge(sem("last_stored"), 16)

        @block.gpsimd
        def _(pool):
            pool.memset(ident[:, :], 0.0).then_inc(sem("pool_const"), 1)
            pool.memset(node_on[:, :], 1.0).then_inc(sem("pool_const"), 1)
            pool.memset(half_neg[:, :], -0.5).then_inc(sem("pool_const"), 1)
            pool.memset(w0T2[:, :], 0.0).then_inc(sem("w0T2_cleared"), 1)
            pool.memset(shifted[0:1, :], 0.0).then_inc(sem("shift_cleared"), 1)
            pool.wait_ge(sem("pool_const"), 3)
            pool.affine_select(out=ident[:, :], in_=ident[:, :], compare_op=ALU.not_equal, fill=1.0,
                               base=0, pattern=[[-1, P]], channel_multiplier=1).then_inc(sem("pool_const"), 1)
            pool.memset(node_on[0:1, 0:1], 0.0).then_inc(sem("pool_const"), 1)
            pool.wait_ge(sem("pool_const"), 5)
            pool.tensor_copy(ident16[:, :], ident[:, :]).then_inc(sem("pool_const"), 1)
            pool.tensor_copy(ident_h[:, :], ident[:, :]).then_inc(sem("pool_const"), 1)
            pool.wait_ge(sem("x_loaded"), 16 * B)
            with strided(pool, 0, NT, 2) as t:
                for u in range(2):
                    pool.wait_ge(sem("xT"), t + u)
                    gate(pool, "pool")
                    pool.tensor_copy(pair(work[:, u, :]), x_btc[:, :, t + u, :]).then_inc(sem("x_staged"), 1)
            with strided(pool, 0, NT, 2) as i:
                for v in range(2):
                    w = slice(v * B, (v + 1) * B)
                    pool.wait_ge(sem("a_var"), i + v + 1)
                    gate(pool, "pool")
                    pool.tensor_tensor(small[:, 3, w], small[:, 2, w], half_neg[:, 0:B], ALU.pow).then_inc(sem("a_rstd"), 1)
            pool.wait_ge(sem("x1_done"), NT)

            def part_step(k, u):
                since(pool, sem("p1_xT"), k - 1)
                gate(pool, "pool")
                x1 = col(xs, k, G * D).rearrange("p (s c) -> p s c", s=G)
                pool.tensor_copy(x_parts(u)[:, :, 0, :], x1).then_inc(sem("x1_hi"), 1)
                pool.wait_ge(sem("x1_hi"), k + 1)
                gate(pool, "pool")
                pool.tensor_tensor(x_parts(u)[:, :, 1, :], x1, x_parts(u)[:, :, 0, :], ALU.subtract).then_inc(sem("x1_lo"), 1)

            units(pool, part_step)

            with pool.Fori(0, B) as b:
                for h in range(H):
                    i = b * H + h
                    z = outs[:, h % 2, :]
                    zv = z.rearrange("p (t d) -> p t d", t=NT)
                    parts = z_parts.rearrange("p (t k d) -> p t k d", t=NT, k=2)
                    pool.wait_ge(sem("out_copied"), (i + 1) * NT)
                    gate(pool, "pool")
                    pool.wait_ge(sem("inverse"), (i + 1) * NT)
                    gate(pool, "pool")
                    pool.tensor_tensor(zv, zv, row_inv[:, h % 2, :].rearrange("p (t o) -> p t o", o=1).to_broadcast([P, NT, D]),
                                       ALU.mult).then_inc(sem("z_scaled"), 1)
                    pool.wait_ge(sem("z_scaled"), i + 1)
                    gate(pool, "pool")
                    pool.tensor_tensor(zv, zv, bh_rows[:, h:h + 1, :].to_broadcast([P, NT, D]), ALU.add).then_inc(sem("z_biased"), 1)
                    pool.wait_ge(sem("z_biased"), i + 1)
                    gate(pool, "pool")
                    pool.wait_ge(sem("z_stored"), i * 16)
                    gate(pool, "pool")
                    pool.tensor_scalar(scratch[:, :], z, 0.0, -0.8, ALU.min, ALU.mult).then_inc(sem("z_less"), 1)
                    pool.wait_ge(sem("z_less"), i + 1)
                    gate(pool, "pool")
                    pool.tensor_tensor(z, z, scratch[:, :], ALU.add).then_inc(sem("z_leaky"), 1)
                    pool.wait_ge(sem("z_leaky"), i + 1)
                    gate(pool, "pool")
                    pool.tensor_copy(parts[:, :, 0, :], zv).then_inc(sem("z_hi"), 1)
                    pool.wait_ge(sem("z_hi"), i + 1)
                    gate(pool, "pool")
                    pool.tensor_tensor(parts[:, :, 1, :], zv, parts[:, :, 0, :], ALU.subtract).then_inc(sem("outs_taken"), 1)
                    pool.wait_ge(sem("outs_taken"), i + 1)
                    gate(pool, "pool")
                    pool.dma_start(z_d[:, bass.ds(i, 1), :], z_parts).then_inc(sem("z_stored"), 16)

            def half_batch(b, u, half):
                c = 2 * b + half
                pool.wait_ge(sem("out_copied"), (b + LAYER1) * NT + (half + 1) * (NT // 2))
                pool.wait_ge(sem("inverse"), (b + LAYER1) * NT + (half + 1) * (NT // 2))
                gate(pool, "pool")
                finish(pool, c, u, half, "f")
                pool.dma_start(half_out(b, half), half_x1(c)).then_inc(sem("out_stored"), 16)

            pool.wait_ge(sem("z_stored"), 16 * LAYER1)
            with strided(pool, 0, B - 2, 2) as b:
                for u in range(2):
                    for half in range(2):
                        half_batch(b + u, u, half)
            half_batch(B - 2, 0, 0)
            half_batch(B - 2, 0, 1)
            half_batch(B - 1, 1, 0)
            for k in range(2):
                pool.wait_ge(sem("last_var"), k + 1)
                pool.tensor_tensor(stats[:, 2, :], stats[:, 1, :], half_neg[:, 0:NT // 2], ALU.pow).then_inc(sem("last_rstd"), 1)
            pool.wait_ge(sem("out_stored"), 16 * (2 * B - 1))

        @block.tensor
        def _(pe):
            pe.wait_ge(sem("pool_const"), 7)
            pe.wait_ge(sem("weights_loaded"), 16 * 9)
            pe.transpose(ps[0:D, 0, 0:D], w_nat[0:D, 0:D], ident[0:D, 0:D])
            for k in range(2):
                pe.transpose(ps[0:D, 0, D + k * P:D + (k + 1) * P], w_nat[:, D + k * D:D + (k + 1) * D], ident[:, :])
            for k in range(H):
                last = pe.transpose(ps[0:D, 1, k * D:(k + 1) * D], w_nat[0:D, 3 * D + k * D:3 * D + (k + 1) * D], ident[0:D, 0:D])
            last.then_inc(sem("weights_turned"), 1)
            for q in range(4):
                for j in range(4):
                    last = pe.transpose(ps[:, 2 + q, j * P:(j + 1) * P],
                                        a_in.rearrange("f (p t) -> f t p", t=NT)[:, 4 * q + j, :], ident[:, :])
                last.then_inc(sem("a_turned"), 1)
            pe.wait_ge(sem("weights_copied"), 2)
            pe.wait_ge(sem("a_copied"), 4)
            with strided(pe, 0, NT, 2) as t:
                for u in range(2):
                    pe.wait_ge(sem("x_staged"), t + u + 1)
                    for k in range(4):
                        last = pe.transpose(ps[:, 4 + u, k * P:(k + 1) * P], work[:, u, k * P:(k + 1) * P], ident[:, :])
                    last.then_inc(sem("xT"), 1)
                    pe.wait_ge(sem("xT_copied"), t + u + 1)
                    pe.wait_ge(sem("h32"), t + u)
                    for k in range(4):
                        last = pe.matmul(ps[:, 6 + u, k * P:(k + 1) * P], work2[:, u, k * P:(k + 1) * P], w0T2[:, :], start=True, stop=True)
                    last.then_inc(sem("h_ready"), 1)
            pe.wait_ge(sem("hi_made"), NT)
            pe.wait_ge(sem("lo_made"), NT)
            pe.wait_ge(sem("ones_made"), 1)
            for t in range(NT):
                pe.matmul(ps[:, 4, :], ones16, h_hi[:, t * BD:(t + 1) * BD], start=(t == 0), stop=False)
                last = pe.matmul(ps[:, 4, :], ones16, h_lo[:, t * BD:(t + 1) * BD], start=False, stop=(t == NT - 1))
            last.then_inc(sem("hsum_ready"), 1)
            pe.wait_ge(sem("shifted_in"), 16 * 4)
            pe.wait_ge(sem("hsum_copied"), 1)
            with strided(pe, 0, NT // 4, 2) as sweep:
                for u in range(2):
                    pe.wait_ge(sem("neigh_free"), 4 * (sweep + u) + 4)
                    pe.wait_ge(sem("mask_made"), 1)

                    def products(t, hi, lo, start, stop):
                        for j in range(4):
                            m = mask[:, bass.ds(t * N + (sweep + u) * (4 * P) + j * P, P)]
                            pe.matmul(ps[:, 4 * u + j, :], m, hi, start=start, stop=False)
                            last = pe.matmul(ps[:, 4 * u + j, :], m, lo, start=False, stop=stop)
                        return last

                    products(0, shifted[:, 0:BD], shifted[:, BD:2 * BD], True, False)
                    with pe.Fori(1, NT - 1) as t:
                        pe.wait_ge(sem("mask_made"), t + 1)
                        products(t, h_hi[:, bass.ts(t - 1, BD)], h_lo[:, bass.ts(t - 1, BD)], False, False)
                    pe.wait_ge(sem("mask_made"), NT)
                    products(NT - 1, h_hi[:, (NT - 2) * BD:(NT - 1) * BD], h_lo[:, (NT - 2) * BD:(NT - 1) * BD],
                             False, True).then_inc(sem("neigh_ready"), 1)
            def turn_x1(k, u):
                since(pe, sem("x1_lo"), k + 1)
                since(pe, sem("p1_xT_copied"), k - 1)
                for s in range(G):
                    last = pe.transpose(banks16(u, 1)[:, s * P:(s + 1) * P],
                                        x_parts(u).rearrange("p s k c -> p s (k c)")[:, s, :], ident_h[:, :])
                last.then_inc(sem("p1_xT"), 1)

            def turn_h(k, u):
                pe.wait_ge(sem("p1_lo"), k + 1)
                since(pe, sem("p1_hT_a"), k)
                since(pe, sem("p1_hT_b"), k)
                for c in range(H * G):
                    last = pe.transpose(banks16(6, 2)[:, c * P:(c + 1) * P], h_parts(u)[:, c * P:(c + 1) * P], ident_h[:, :])
                last.then_inc(sem("p1_hT"), 1)

            def p1_step(k, u):
                pe.wait_ge(sem("p1_xT_copied"), k + 1)
                since(pe, sem("p1_lo"), k - 1)
                for s in range(G):
                    o = ps[:, 2 + 2 * u + s // 2, (s % 2) * H * D:(s % 2 + 1) * H * D]
                    for part in range(2):
                        last = pe.matmul(o, xT_parts(u)[:, s * P:(s + 1) * P], w16[:, 0, part, :], start=(part == 0), stop=(part == 1))
                last.then_inc(sem("p1_h"), 1)
                if within(k + 1):
                    turn_x1(k + 1, 1 - u)
                if within(k - 1):
                    turn_h(k - 1, 1 - u)

            pe.wait_ge(sem("x1_done"), NT)
            turn_x1(0, 0)
            units(pe, p1_step)
            turn_h(UNITS - 1, 1)

            def step(g, u, instance, t, parity, tile):
                def half(c):
                    since(pe, sem(f"masked{c}"), g)
                    for q in range(2):
                        o = ps[:, 2 * c + q, :]
                        w = slice((2 * c + q) * BANK, (2 * c + q + 1) * BANK)
                        k = col(k_both[:, parity], t, P)
                        pe.matmul(o, k, q_head[:, parity, w], start=True, stop=False)
                        last = pe.matmul(o, k, q_tail[:, parity, w], start=False, stop=True)
                    last.then_inc(sem(f"scores{c}"), 1)

                new, old = tile(1), tile(2)

                def turn(q, slot):
                    for j in range(4):
                        c = 4 * q + j
                        last = pe.matmul(ps[:, TURN_BANK[q], j * P:(j + 1) * P], probs[:, slot, c * P:(c + 1) * P], ident[:, :],
                                         start=(j == 0), stop=(j == 3), is_transpose=True, skip_group_check=True)
                    last.then_inc(sem(f"turned{q}"), 1)

                def weigh(q, lag):
                    pe.wait_ge(sem(f"part_lo{q}"), g - lag + 1)
                    slot, held = (u - lag) % 2, tile(lag)[0]
                    for j in range(4):
                        c = 4 * q + j
                        w, v, v_tail = slice(j * P, (j + 1) * P), slice(c * P, c * P + D), slice(c * P + D, (c + 1) * P)
                        hi, lo = probsT_hi[:, slot, q, w], probsT_lo[:, slot, q, w]
                        pe.matmul(ps[:, 7, 0:D], hi, v_parts[:, held, v], start=(c == 0), stop=False)
                        pe.matmul(ps[:, 7, 0:D], hi, v_parts[:, held, v_tail], start=False, stop=False)
                        last = pe.matmul(ps[:, 7, 0:D], lo, v_parts[:, held, v], start=False, stop=(c == NT - 1))
                    return last

                if t is not None:
                    if isinstance(t, int) and t == 0:
                        pe.wait_ge(sem(f"operands{parity}"), (instance - parity) * (8 * OPERAND_DMAS) + 16 * OPERAND_DMAS)
                    half(0)
                if old:
                    pe.wait_ge(sem("part_lo1"), g - 1)
                    turn(3, u)
                if t is not None:
                    half(1)
                if new:
                    pe.wait_ge(sem("exp_done"), g)
                    since(pe, sem("part_lo0"), g - 1)
                    turn(0, 1 - u)
                if tile(3):
                    weigh(2, 3)
                    weigh(3, 3).then_inc(sem("weighed"), 1)
                if new:
                    since(pe, sem("part_lo3"), g - 1)
                    turn(1, 1 - u)
                    since(pe, sem("part_lo2"), g - 1)
                    turn(2, 1 - u)
                if old:
                    since(pe, sem("out_copied"), g - 2)
                    weigh(0, 2)
                    weigh(1, 2)

            attention(0, LAYER1, pe, step, 4)
            def turn_z(k, u):
                pe.wait_ge(sem(f"z_in{u}"), (k - u) * 8 + 16)
                since(pe, sem("p2_zT_a"), k - 1)
                since(pe, sem("p2_zT_b"), k - 1)
                for c in range(H * G):
                    last = pe.transpose(banks16(2 * u, 2)[:, c * P:(c + 1) * P], z_in(u)[:, c * P:(c + 1) * P], ident_h[:, :])
                last.then_inc(sem("p2_zT"), 1)

            def turn_h2(k, u):
                pe.wait_ge(sem("p2_lo"), k + 1)
                since(pe, sem("p2_hT"), k - 1)
                for s in range(G):
                    last = pe.transpose(banks16(6 + u, 1)[:, s * P:(s + 1) * P], h_parts(u)[:, s * P:(s + 1) * P], ident_h[:, :])
                last.then_inc(sem("p2_turned"), 1)

            def p2_step(k, u):
                pe.wait_ge(sem("p2_zT_a"), k + 1)
                pe.wait_ge(sem("p2_zT_b"), k + 1)
                since(pe, sem("p2_lo"), k - 1)
                for s in range(G):
                    for h in range(H):
                        for part in range(2):
                            last = pe.matmul(ps[:, 4 + u, s * D:(s + 1) * D], zT_parts(u)[:, (h * G + s) * P:(h * G + s + 1) * P],
                                             w16[:, 1, part, h * D:(h + 1) * D],
                                             start=(h == 0 and part == 0), stop=(h == H - 1 and part == 1))
                last.then_inc(sem("p2_h"), 1)
                if within(k + 1):
                    turn_z(k + 1, 1 - u)
                if within(k - 1):
                    turn_h2(k - 1, 1 - u)

            turn_z(0, 0)
            units(pe, p2_step)
            turn_h2(UNITS - 1, 1)
            attention(LAYER1, INSTANCES, pe, step, 4)

        @block.scalar
        def _(act):
            act.wait_ge(sem("a_turned"), 4)
            for q in range(4):
                act.copy(aT[:, 4 * q:4 * q + 4, :], ps[:, 2 + q, :].rearrange("p (j n) -> p j n", j=4)).then_inc(sem("a_copied"), 1)
            with strided(act, 0, NT, 2) as t:
                for u in range(2):
                    act.wait_ge(sem("xT"), t + u + 1)
                    act.wait_ge(sem("h_ready"), t + u)
                    act.copy(work2[:, u, :], ps[:, 4 + u, :]).then_inc(sem("xT_copied"), 1)
                    act.wait_ge(sem("h32"), t + u + 1)
                    act.activation(h_hi[:, bass.ts(t + u, BD)], h32[:, u * BD:(u + 1) * BD], ACT.Copy,
                                   scale=node_on[:, bass.ds(t + u, 1)]).then_inc(sem("hi_made"), 1)
            act.wait_ge(sem("hsum_ready"), 1)
            act.copy(hsum[:, :], ps[:, 4, :]).then_inc(sem("hsum_copied"), 1)
            with strided(act, 0, NT, 2) as i:
                for v in range(2):
                    act.wait_ge(sem("a_centred"), i + v + 1)
                    act.square(a_work[v][:, 3, :], a_work[v][:, 2, :]).then_inc(sem("a_squared"), 1)
            def copy_xT(k, u):
                act.wait_ge(sem("p1_xT"), k + 1)
                since(act, sem("p1_h"), k - 1)
                act.copy(xT_parts(u), banks16(u, 1)[:, 0:G * P]).then_inc(sem("p1_xT_copied"), 1)

            def copy_hT(k, u):
                act.wait_ge(sem("p1_hT"), k + 1)
                since(act, sem(f"hT_stored{u}"), stores(k, u))
                act.copy(hT_parts(u)[:, 0:2 * G * P], banks16(6, 1)).then_inc(sem("p1_hT_a"), 1)

            def p1_step(k, u):
                act.wait_ge(sem("p1_h"), k + 1)
                since(act, sem("p1_hT"), k - 1)
                since(act, sem(f"h_stored{u}"), stores(k, u))
                act.copy(by_tiles(h_parts(u), 0), products(u)).then_inc(sem("p1_hi"), 1)
                if within(k + 1):
                    copy_xT(k + 1, 1 - u)
                if within(k - 1):
                    copy_hT(k - 1, 1 - u)

            copy_xT(0, 0)
            units(act, p1_step)
            copy_hT(UNITS - 1, 1)

            def step(g, u, instance, t, parity, tile):
                if isinstance(t, int) and t == 2:
                    outs_free(act, instance)
                if tile(1):
                    old, tt = tile(1)
                    act.wait_ge(sem("masked1"), g)
                    since(act, sem("turned3"), g - 2)
                    act.activation(probs[:, 1 - u, :], scores[:, 1 - u, :], ACT.Exp, bias=neg_max[:, 1 - u:2 - u], scale=-1.0,
                                   accum_out=col(row_sum[:, old], tt)).then_inc(sem("exp_done"), 1)
                def head(q, slot, n):
                    act.wait_ge(sem(f"turned{q}"), n)
                    act.activation(probsT_hi[:, slot, q, :], ps[:, TURN_BANK[q], :], ACT.Copy, scale=SCALE).then_inc(sem(f"part_hi{q}"), 1)

                if tile(2):
                    head(3, u, g - 1)
                if tile(1):
                    head(0, 1 - u, g)
                if tile(3):
                    old, tt = tile(3)
                    act.wait_ge(sem("weighed"), g - 2)
                    act.activation(col(outs[:, old], tt, D), ps[:, 7, 0:D], ACT.Copy, scale=1.0 / SCALE).then_inc(sem("out_copied"), 1)
                if tile(1):
                    head(1, 1 - u, g)
                    head(2, 1 - u, g)
            attention(0, LAYER1, act, step, 4)
            def copy_zT(k, u):
                act.wait_ge(sem("p2_zT"), k + 1)
                since(act, sem("p2_h"), k - 1)
                act.copy(zT_parts(u)[:, 0:2 * G * P], banks16(2 * u, 1)).then_inc(sem("p2_zT_a"), 1)

            def p2_step(k, u):
                act.wait_ge(sem("p2_h"), k + 1)
                since(act, sem("p2_turned"), k - 1)
                since(act, sem(f"h2_stored{u}"), stores(k, u))
                act.copy(tile_part(u, 0), ps[:, 4 + u, 0:G * D].rearrange("p (s d) -> p s d", s=G)).then_inc(sem("p2_hi"), 1)
                if within(k + 1):
                    copy_zT(k + 1, 1 - u)
                if within(k - 1):
                    copy_h2T(k - 1, 1 - u)

            def copy_h2T(k, u):
                act.wait_ge(sem("p2_turned"), k + 1)
                since(act, sem(f"h2T_stored{u}"), stores(k, u))
                act.copy(hT_parts(u)[:, 0:G * P], banks16(6 + u, 1)[:, 0:G * P]).then_inc(sem("p2_hT"), 1)

            copy_zT(0, 0)
            units(act, p2_step)
            copy_h2T(UNITS - 1, 1)
            attention(LAYER1, INSTANCES, act, step, 4)

        @block.vector
        def _(dve):
            dve.sem_inc(sem("neigh_free"), 8)
            dve.wait_ge(sem("weights_loaded"), 16 * 9)
            dve.memset(ones16, 1.0).then_inc(sem("ones_made"), 1)
            dve.wait_ge(sem("weights_turned"), 1)
            dve.wait_ge(sem("w0T2_cleared"), 1)
            for k in range(2):
                dve.tensor_copy(w0T2[k * D:(k + 1) * D, k * D:(k + 1) * D], ps[0:D, 0, 0:D]).then_inc(sem("weights_copied"), 1)
            for k, wT in enumerate((ps[0:D, 0, D:D + H * D], ps[0:D, 1, 0:H * D])):
                for half in range(2):
                    w = slice(half * D, (half + 1) * D)
                    dve.tensor_copy(w16[w, k, 0, :], wT).then_inc(sem("w16_hi"), 1)
                dve.wait_ge(sem("w16_hi"), 2 * k + 2)
                for half in range(2):
                    w = slice(half * D, (half + 1) * D)
                    dve.tensor_tensor(w16[w, k, 1, :], wT, w16[0:D, k, 0, :], ALU.subtract).then_inc(sem("w16_lo"), 1)
            dve.wait_ge(sem("a_copied"), 4)
            b0_all = rows[:, 0:1, :].to_broadcast([P, B, D])
            with strided(dve, 0, NT, 2) as t:
                for u in range(2):
                    dve.wait_ge(sem("h_ready"), t + u + 1)
                    hv = pair(h32[:, u * BD:(u + 1) * BD])
                    dve.tensor_tensor(hv, pair(ps[:, 6 + u, :]), b0_all, ALU.add).then_inc(sem("h32"), 1)
                    dve.wait_ge(sem("h32"), t + u + 1)
                    prod = pair(h32[:, 2 * BD:3 * BD])
                    dve.tensor_tensor(prod, hv, aT[:, bass.ds(t + u, 1), 0:D].to_broadcast([P, B, D]), ALU.mult).then_inc(sem("s1_prod"), 1)
                    dve.wait_ge(sem("s1_prod"), t + u + 1)
                    dve.tensor_reduce(s1[:, t + u, :], prod, AX.X, ALU.add).then_inc(sem("s1_made"), 1)
                    dve.wait_ge(sem("s1_made"), t + u + 1)
                    dve.wait_ge(sem("hi_made"), t + u + 1)
                    dve.scalar_tensor_tensor(h_lo[:, bass.ts(t + u, BD)], h32[:, u * BD:(u + 1) * BD], node_on[:, bass.ds(t + u, 1)],
                                             h_hi[:, bass.ts(t + u, BD)], ALU.mult, ALU.subtract).then_inc(sem("lo_made"), 1)
                    dve.wait_ge(sem(f"adj_loaded{u}"), t * 8 + 16)
                    dve.tensor_scalar(mask[:, bass.ts(t + u, N)].rearrange("p (t q) -> p t q", t=NT),
                                      adj_slot[:, u, :].rearrange("p (q t) -> p t q", t=NT), 0.0, None, ALU.is_gt).then_inc(sem("mask_made"), 1)
            dve.wait_ge(sem("hsum_copied"), 1)
            def over(ap):
                return ap.rearrange("p (b o) -> p b o", o=1).to_broadcast([P, B, D])

            with strided(dve, 0, NT, 8) as i0:
                for j in range(0, 8, 2):
                    if j % 4 == 0:
                        dve.wait_ge(sem("neigh_ready"), i0 // 4 + j // 4 + 1)
                    both = [(v, i0 + j + v, a_work[v], small[:, :, v * B:(v + 1) * B]) for v in range(2)]
                    for v, i, w, sm in both:
                        dve.tensor_tensor(pair(w[:, 0, :]), pair(ps[:, j + v, :]), aT[:, bass.ds(i, 1), D:P].to_broadcast([P, B, D]),
                                          ALU.mult).then_inc(sem("neigh_free"), 1)
                    for v, i, w, sm in both:
                        dve.wait_ge(sem("neigh_free"), i + 9)
                        dve.tensor_reduce(sm[:, 0, :], pair(w[:, 0, :]), AX.X, ALU.add).then_inc(sem("s2_made"), 1)
                    for v, i, w, sm in both:
                        dve.wait_ge(sem("s2_made"), i + 1)
                        dve.tensor_tensor(sm[:, 1, :], sm[:, 0, :], s1[:, i, :], ALU.add).then_inc(sem("s_sum"), 1)
                    for v, i, w, sm in both:
                        dve.wait_ge(sem("s_sum"), i + 1)
                        dve.tensor_scalar(sm[:, 1, :], sm[:, 1, :], node_on[:, bass.ds(i, 1)], None, ALU.mult).then_inc(sem("s_made"), 1)
                    for v, i, w, sm in both:
                        dve.wait_ge(sem("s_made"), i + 1)
                        dve.tensor_tensor(pair(w[:, 0, :]), pair(hsum[:, :]), over(sm[:, 1, :]), ALU.mult).then_inc(sem("hp"), 1)
                    for v, i, w, sm in both:
                        dve.wait_ge(sem("hp"), i + 1)
                        dve.scalar_tensor_tensor(w[:, 1, :], w[:, 0, :], 0.01, w[:, 0, :], ALU.mult, ALU.max).then_inc(sem("hp_leaky"), 1)
                    for v, i, w, sm in both:
                        dve.wait_ge(sem("hp_leaky"), i + 1)
                        dve.tensor_tensor(pair(w[:, 1, :]), pair(w[:, 1, :]), x_btc[:, :, i, :], ALU.add).then_inc(sem("a_y"), 1)
                    for v, i, w, sm in both:
                        dve.wait_ge(sem("a_y"), i + 1)
                        dve.tensor_reduce(sm[:, 0, :], pair(w[:, 1, :]), AX.X, ALU.add).then_inc(sem("a_mean"), 1)
                    for v, i, w, sm in both:
                        dve.wait_ge(sem("a_mean"), i + 1)
                        dve.scalar_tensor_tensor(pair(w[:, 2, :]), over(sm[:, 0, :]), -1.0 / D, pair(w[:, 1, :]),
                                                 ALU.mult, ALU.add).then_inc(sem("a_centred"), 1)
                    for v, i, w, sm in both:
                        dve.wait_ge(sem("a_squared"), i + 1)
                        dve.tensor_reduce(sm[:, 2, :], pair(w[:, 3, :]), AX.X, ALU.add).then_inc(sem("a_ssq"), 1)
                    for v, i, w, sm in both:
                        dve.wait_ge(sem("a_ssq"), i + 1)
                        dve.tensor_scalar(sm[:, 2, :], sm[:, 2, :], 1.0 / D, EPS, ALU.mult, ALU.add).then_inc(sem("a_var"), 1)
                    for v, i, w, sm in both:
                        dve.wait_ge(sem("a_rstd"), i + 1)
                        dve.wait_ge(sem("a_centred"), i + 1)
                        dve.tensor_tensor(x_btc[:, :, i, :], pair(w[:, 2, :]), over(sm[:, 3, :]), ALU.mult).then_inc(sem("x1_done"), 1)
            with dve.Fori(0, NT) as t:
                d = mask[:, bass.ds(t * (N + P), P)]
                dve.tensor_tensor(d, d, ident16[:, :], ALU.max).then_inc(sem("mask_diag"), 1)
                dve.wait_ge(sem("mask_diag"), t + 1)
                m = mask[:, bass.ts(t, N)]
                dve.tensor_scalar(m, m, -1.0, MASKED_SCORE, ALU.add, ALU.mult).then_inc(sem("mask_ready"), 1)
            def copy_hT(k, u):
                dve.wait_ge(sem("p1_hT"), k + 1)
                since(dve, sem(f"hT_stored{u}"), stores(k, u))
                dve.tensor_copy(hT_parts(u)[:, 2 * G * P:4 * G * P], banks16(7, 1)).then_inc(sem("p1_hT_b"), 1)

            def p1_step(k, u):
                dve.wait_ge(sem("p1_hi"), k + 1)
                dve.tensor_tensor(by_tiles(h_parts(u), 1), products(u), by_tiles(h_parts(u), 0), ALU.subtract).then_inc(sem("p1_lo"), 1)
                if within(k - 1):
                    copy_hT(k - 1, 1 - u)

            units(dve, p1_step)
            copy_hT(UNITS - 1, 1)

            def step(g, u, instance, t, parity, tile):
                def masked(c):
                    dve.wait_ge(sem(f"scores{c}"), g + 1)
                    if c == 1:
                        dve.wait_ge(sem("masked0"), g + 1)
                    w = slice(c * 2 * BANK, (c + 1) * 2 * BANK)
                    if c == 0:
                        dve.wait_ge(sem(f"mask_staged{u}"), (g - u) * 8 + 16)
                        since(dve, sem("exp_done"), g - 1)
                    gate(dve, "dve")
                    start = 3.0e38 if c == 0 else neg_max0[:, u:u + 1]
                    dve.tensor_tensor_reduce(scores[:, u, w], ps[:, 2 * c:2 * c + 2, :].rearrange("p a n -> p (a n)"), mask_slot[:, u, w],
                                             -1.0, start, ALU.add, ALU.min,
                                             (neg_max0 if c == 0 else neg_max)[:, u:u + 1]).then_inc(sem(f"masked{c}"), 1)

                def remainder(q, slot, n):
                    dve.wait_ge(sem(f"part_hi{q}"), n)
                    dve.scalar_tensor_tensor(probsT_lo[:, slot, q, :], ps[:, TURN_BANK[q], :], SCALE, probsT_hi[:, slot, q, :],
                                             ALU.mult, ALU.subtract).then_inc(sem(f"part_lo{q}"), 1)

                if t is not None:
                    masked(0)
                if tile(2):
                    remainder(3, u, g - 1)
                if t is not None:
                    masked(1)
                if tile(1):
                    for q in range(3):
                        remainder(q, 1 - u, g)
                if isinstance(t, int) and t == 1:
                    outs_free(dve, instance)
                if tile(1):
                    new, tt = tile(1)
                    dve.wait_ge(sem("exp_done"), g)
                    dve.reciprocal(col(row_inv[:, new], tt), col(row_sum[:, new], tt)).then_inc(sem("inverse"), 1)

            attention(0, LAYER1, dve, step)
            def copy_zT(k, u):
                dve.wait_ge(sem("p2_zT"), k + 1)
                since(dve, sem("p2_h"), k - 1)
                dve.tensor_copy(zT_parts(u)[:, 2 * G * P:4 * G * P], banks16(2 * u + 1, 1)).then_inc(sem("p2_zT_b"), 1)

            def p2_step(k, u):
                dve.wait_ge(sem("p2_hi"), k + 1)
                dve.tensor_tensor(tile_part(u, 1), ps[:, 4 + u, 0:G * D].rearrange("p (s d) -> p s d", s=G), tile_part(u, 0),
                                  ALU.subtract).then_inc(sem("p2_lo"), 1)
                if within(k + 1):
                    copy_zT(k + 1, 1 - u)

            copy_zT(0, 0)
            units(dve, p2_step)

            attention(LAYER1, INSTANCES, dve, step)
            dve.wait_ge(sem("out_copied"), INSTANCES * NT)
            dve.wait_ge(sem("inverse"), INSTANCES * NT)
            dve.wait_ge(sem("f_done"), 2 * B - 1)
            finish(dve, 2 * B - 1, 1, 1, "last")


_INS = ['x', 'adj', 'L0_gnn_W_w', 'L0_gnn_W_b', 'L0_gnn_a', 'L1_gnn_Wh', 'L1_gnn_bh', 'L1_gnn_Wo', 'L1_gnn_bo',
        'L1_gnn_gamma', 'L1_gnn_beta']


def kernel(**inputs):
    import numpy as _np
    import concourse.bacc as _bacc
    from concourse import mybir as _mybir
    from concourse.bass_utils import run_bass_kernel_spmd as _run

    nc = _bacc.Bacc("TRN2", target_bir_lowering=False, num_devices=1)
    arrays, args = {}, []
    for name in _INS:
        v = _np.ascontiguousarray(inputs[name])
        arrays[f"in_{name}"] = v
        args.append(nc.dram_tensor(f"in_{name}", v.shape, _mybir.dt.from_np(v.dtype), kind="ExternalInput").ap())
    args.append(nc.dram_tensor("out_0", (B, N, D), F32, kind="ExternalOutput").ap())
    build(nc, *args)
    r = _run(nc, [arrays], core_ids=[0])
    return r.results[0]["out_0"]
```
